# Optimizing a Trainium2 kernel written in Bass

```python
import numpy as np
import jax
import jax.numpy as jnp

def _softmax(x, axis=-1):
    return jax.nn.softmax(x, axis=axis)

def _gelu(x):
    return jax.nn.gelu(x, approximate=True)

def _silu(x):
    return jax.nn.silu(x)

def _sigmoid(x):
    return jax.nn.sigmoid(x)

def _layernorm(x, axis=-1, eps=1e-05):
    m = jnp.mean(x, axis=axis, keepdims=True)
    v = jnp.var(x, axis=axis, keepdims=True)
    return (x - m) / jnp.sqrt(v + eps)

def _scatter_add(tgt, idx, src, axis=0):
    return tgt.at[idx].add(src)

def _segment_sum(src, seg, n):
    return jax.ops.segment_sum(src, seg, n)
kernel_name = 'mk_adaln_d1_jaxref_r8_cde214'

def setup_inputs(seed: int=0):
    np.random.seed(seed)
    _w = jnp.asarray

    def _L0_attn_setup():
        import math
        import jax, jax.numpy as jnp
        import numpy as np
        N_HEADS = 16
        D_EMBED = 128
        key = jax.random.key(seed)
        ks = jax.random.split(key, 5)
        b, l, d = (2, 256, D_EMBED)
        return {'x': jax.random.normal(ks[0], (b, l, d), dtype=jnp.float32), 'w_in': jax.random.normal(ks[1], (3 * d, d), dtype=jnp.float32) * 0.02, 'b_in': jax.random.normal(ks[2], (3 * d,), dtype=jnp.float32) * 0.02, 'w_out': jax.random.normal(ks[3], (d, d), dtype=jnp.float32) * 0.02, 'b_out': jax.random.normal(ks[4], (d,), dtype=jnp.float32) * 0.02}
    _L0_attn_in = _L0_attn_setup()

    def _L0_ffn_setup():
        import jax, jax.numpy as jnp
        import numpy as np
        B, S, D, E, F = (2, 256, 128, 14, 256)
        key = jax.random.key(seed)
        k = jax.random.split(key, 4)
        h = jax.random.normal(k[0], (B, S, D), dtype=jnp.float32)
        router_w = jax.random.normal(k[1], (D, E), dtype=jnp.float32) * 0.02
        w1 = jax.random.uniform(k[2], (E, D, F), dtype=jnp.float32, minval=-1.0, maxval=1.0) * float(np.sqrt(6.0 / D))
        w2 = jax.random.uniform(k[3], (E, F, D), dtype=jnp.float32, minval=-1.0, maxval=1.0) * float(np.sqrt(6.0 / F))
        b1 = jnp.zeros((E, F), dtype=jnp.float32)
        b2 = jnp.zeros((E, D), dtype=jnp.float32)
        return {'h': h, 'router_w': router_w, 'w1': w1, 'b1': b1, 'w2': w2, 'b2': b2}
    _L0_ffn_in = _L0_ffn_setup()
    _L0_c = _w((lambda *s: np.random.randn(*s).astype(np.float32) * 0.05)(32, 128))
    _L0_wmod = _w((lambda *s: np.random.randn(*s).astype(np.float32) * 0.05)(128, 6 * 128) * 128 ** (-0.5))
    _d = {'L0_attn_x': _L0_attn_in['x'], 'L0_attn_w_in': _L0_attn_in['w_in'], 'L0_attn_b_in': _L0_attn_in['b_in'], 'L0_attn_w_out': _L0_attn_in['w_out'], 'L0_attn_b_out': _L0_attn_in['b_out'], 'L0_ffn_router_w': _L0_ffn_in['router_w'], 'L0_ffn_w1': _L0_ffn_in['w1'], 'L0_ffn_b1': _L0_ffn_in['b1'], 'L0_ffn_w2': _L0_ffn_in['w2'], 'L0_ffn_b2': _L0_ffn_in['b2'], 'L0_c': _L0_c, 'L0_wmod': _L0_wmod}
    _x0 = _d['L0_attn_x']
    _d['L0_attn_x'] = jax.random.normal(jax.random.fold_in(jax.random.key(seed), 1), (32, 256, 128), dtype=_x0.dtype)
    del _x0
    return _d

def reference(L0_attn_x, L0_attn_w_in, L0_attn_b_in, L0_attn_w_out, L0_attn_b_out, L0_ffn_router_w, L0_ffn_w1, L0_ffn_b1, L0_ffn_w2, L0_ffn_b2, L0_c, L0_wmod):

    def _L0_attn_ref(x, w_in, b_in, w_out, b_out):
        import math
        import jax, jax.numpy as jnp
        import numpy as np
        N_HEADS = 16
        D_EMBED = 128
        b, l, d = x.shape
        h = N_HEADS
        scale = 1.0 / math.sqrt(d // h)
        x_proj = (x @ w_in.T + b_in).reshape(b, l, h, -1)
        q, k, v = jnp.split(x_proj, 3, axis=-1)
        att = jnp.einsum('blhd,bmhd->blmh', q, k) * scale
        att = jax.nn.softmax(att, axis=2)
        opt = jnp.einsum('blmh,blhd->blhd', att, v).reshape(b, l, d)
        return opt @ w_out.T + b_out

    def _L0_ffn_ref(h, router_w, w1, b1, w2, b2):
        import jax, jax.numpy as jnp
        import numpy as np
        B, S, D, E, F = (2, 256, 128, 14, 256)
        Bb, Ss, Dd = h.shape
        x = h.reshape(-1, Dd)
        logits = x @ router_w
        assignments = jnp.argmax(logits, axis=-1)
        probs = jax.nn.softmax(logits, axis=-1)
        weights = jnp.take_along_axis(probs, assignments[:, None], axis=1)[:, 0]
        hid = jnp.einsum('nd,edf->nef', x, w1) + b1
        hid = jax.nn.gelu(hid, approximate=False)
        all_out = jnp.einsum('nef,efd->ned', hid, w2) + b2
        sel = jnp.take_along_axis(all_out, assignments[:, None, None], axis=1)[:, 0, :]
        moe_out = (sel * weights[:, None]).reshape(Bb, Ss, Dd)
        return moe_out
    x = L0_attn_x
    mod = (_silu(L0_c) @ L0_wmod).reshape(L0_c.shape[0], 6, 1, -1)
    sa, ca, ga, sb, cb, gb = (mod[:, 0], mod[:, 1], mod[:, 2], mod[:, 3], mod[:, 4], mod[:, 5])
    ga = (2 * (ga >= 0) - 1) * jnp.maximum(jnp.abs(ga), 0.25)
    gb = (2 * (gb >= 0) - 1) * jnp.maximum(jnp.abs(gb), 0.25)
    h = _layernorm(x, axis=-1) * (1 + ca) + sa
    x = x + ga * _L0_attn_ref(h, L0_attn_w_in, L0_attn_b_in, L0_attn_w_out, L0_attn_b_out)
    h = _layernorm(x, axis=-1) * (1 + cb) + sb
    x = x + gb * _L0_ffn_ref(h, L0_ffn_router_w, L0_ffn_w1, L0_ffn_b1, L0_ffn_w2, L0_ffn_b2)
    return x

_drawn_inputs = setup_inputs


def setup_inputs(seed=0):
    import zlib

    import numpy as np

    out = dict(_drawn_inputs(seed))
    spreads = {'L0_ffn_b1': (0.0, 2.0), 'L0_ffn_b2': (0.0, 2.0)}
    factors = {'L0_attn_w_in': 4.175, 'L0_attn_b_in': 8.0, 'L0_attn_w_out': 4.152, 'L0_attn_b_out': 8.0}
    for name, (base, spread) in spreads.items():
        noise = np.random.default_rng([zlib.crc32(name.encode()), seed]).standard_normal(out[name].shape)
        drawn = base * np.exp(spread * noise) if base else spread * noise
        out[name] = jnp.asarray(drawn.astype(out[name].dtype))
    for name, factor in factors.items():
        out[name] = (out[name] * factor).astype(out[name].dtype)
    return out
```

```python
from contextlib import ExitStack

import concourse.bass as bass
from concourse import mybir
from concourse.alu_op_type import AluOpType as ALU

F32 = mybir.dt.float32
BF16 = mybir.dt.bfloat16
I32 = mybir.dt.int32
ACT = mybir.ActivationFunctionType
AX_X = mybir.AxisListType.X
ds = bass.ds

P = 128
D = 128
B = 32
L = 256
LT = L // P
T = B * LT
NTOK = B * L
H = 16
DH = D // H
E = 14
F = 256
FH = F // P
SCALE = float(DH) ** -0.5
EPS = 1e-5

HU = 4
UNITS = LT * H // HU
RING = 3
BUF_OF = [u % RING for u in range(UNITS)]
BACK = [next(k for k in range(1, 2 * UNITS) if BUF_OF[(u - k) % UNITS] == BUF_OF[u]) for u in range(UNITS)]

Q_PART = [0, 1, 2, 0, 1, 0]
K_PART = [0, 0, 0, 1, 1, 2]
COMBOS = len(Q_PART)

ROOM = NTOK + P
PAD_AT = E * ROOM
H2, X2, GW, ID = 0, D, 2 * D, 3 * D
ROW = 3 * D + 1
NO_TOKEN = float(1 << 20)

SLOTS = 8
NT = -(-(T + E - 1) // SLOTS) * SLOTS
W1X = F + FH

X_CHUNKS = [(0, 1), (1, 2), (2, 4), (4, B)]

MODROWS = 5


def need(eng, sem, value):
    if isinstance(value, int) and value <= 0:
        return
    eng.wait_ge(sem, value)


class Steps:

    def __init__(self, eng, sem, held):
        self.eng, self.sem, self.held, self.base, self.n = eng, sem, held, 0, 0

    def then(self, ins, plain=False):
        self.n += 1
        ins.then_inc(self.sem, 1)
        self.eng.wait_ge(self.sem, self.base + self.n)
        if plain:
            self.plain()

    def plain(self):
        self.eng.sem_inc(self.held, 1)

    def enter(self, i, per_turn):
        self.start = self.base + self.n
        self.base, self.n, self.per_turn = self.start + i * per_turn, 0, per_turn

    def leave(self, turns):
        assert self.n == self.per_turn, self.n
        self.base, self.n = self.start + turns * self.per_turn, 0


PEELED = 4
STEPS_POOL = 10
STEPS_DVE = 14


def over_batches(eng, iteration, drain, steps=None, per_turn=0, before_loop=None):
    for b in range(PEELED):
        iteration(b, b % 2)
    turns = (B - PEELED - 4) // 2
    if before_loop:
        before_loop()
    with eng.Fori(0, turns) as i:
        if steps:
            steps.enter(i, per_turn)
        iteration(2 * i + PEELED, 0)
        iteration(2 * i + PEELED + 1, 1)
    if steps:
        steps.leave(turns)
    for b in range(PEELED + 2 * turns, B):
        iteration(b, b % 2)
    drain(B, 0)


def has_tail(b):
    return not (isinstance(b, int) and b < 1)


def has_routing(b):
    return not (isinstance(b, int) and b < 2)


def has_norm(b):
    return not (isinstance(b, int) and b + 3 >= B)


def has_prep(b):
    return not (isinstance(b, int) and b + 2 >= B)


def over_tiles(eng, step, lag, steps=None, per_turn=0):
    for s in range(SLOTS):
        step(s, s, 0)
    turns = NT // SLOTS - 1
    with eng.Fori(0, turns) as i:
        if steps:
            steps.enter(i, per_turn)
        for s in range(SLOTS):
            step(SLOTS * i + SLOTS + s, s, i + 1)
    if steps:
        steps.leave(turns)
    for s in range(lag):
        step(NT + s, s, turns + 1)


def build_adaln_attention_moe(nc, x, w_qkv, b_qk, b_v, w_out, b_out, router_w, w1x, w2, b2, c_t, wmod,
                              ident, before, expert_row, first_row, tile_numbers, token_numbers, out):
    with ExitStack() as ctx:
        def sb(name, shape, dt=F32):
            return ctx.enter_context(nc.sbuf_tensor(name, shape, dt))

        def ps(name, shape, dt=F32):
            return ctx.enter_context(nc.psum_tensor(name, shape, dt))

        def sem(name):
            return ctx.enter_context(nc.semaphore(name))

        def dram(name, shape, dt=F32):
            return nc.dram_tensor(name, shape, dt, kind="Internal").ap()

        mod_rows = dram("mod_rows", (B, MODROWS * D))
        parts_dram = dram("parts_dram", (2, 2, 3, P, L), BF16)
        table = dram("table", (PAD_AT + P, ROW))

        x_tiles = x.rearrange("b (t p) d -> p (b t) d", p=P)
        out_rows = out.rearrange("b l d -> (b l) d")

        ident_s = sb("ident_s", [P, P])
        before_s = sb("before_s", [P, P], BF16)
        before_f = sb("before_f", [P, P])
        ones_s = sb("ones_s", [P, P], BF16)
        w_qkv_s = sb("w_qkv_s", [P, 3, D])
        b_qk_s = sb("b_qk_s", [P, 2])
        b_v_s = sb("b_v_s", [P, D])
        w_out_s = sb("w_out_s", [P, D])
        b_out_s = sb("b_out_s", [B, D])
        router_s = sb("router_s", [P, E])
        w1x_s = sb("w1x_s", [P, E, W1X])
        w2_s = sb("w2_s", [P, E, FH, D])
        b2_s = sb("b2_s", [P, E, D])
        expert_s = sb("expert_s", [P, 3, E])
        c_s = sb("c_s", [P, B])
        silu_s = sb("silu_s", [P, 3, B])
        wmod_s = sb("wmod_s", [P, 6 * D])
        mod_s = sb("mod_s", [B, 6 * D])
        rows_out = sb("rows_out", [B, MODROWS, D])
        mod_tmp = sb("mod_tmp", [B, 3, 2 * D])
        shift_a = sb("shift_a", [P, B])
        scale_a = sb("scale_a", [P, B])
        minus_half = sb("minus_half", [P, LT])
        eps_s = sb("eps_s", [P, LT])
        batch_s = sb("batch_s", [P, LT], I32)
        centred1 = sb("centred1", [P, LT, D])
        centred2 = sb("centred2", [P, LT, D])
        pad_tile = sb("pad_tile", [P, ROW])
        x_s = sb("x_s", [P, T, D])
        v_s = sb("v_s", [P, T, D])
        q_stack = [sb(f"q_stack{p}", [P, H, L], BF16) for p in range(2)]
        k_stack = [sb(f"k_stack{p}", [P, H, L], BF16) for p in range(2)]
        bn1 = sb("bn1", [P, LT, 6])
        mv1 = sb("mv1", [P, LT, 2])
        rstd1 = sb("rstd1", [P, 2, LT])
        xhat1 = sb("xhat1", [P, LT, D])
        h_t = sb("h_t", [P, L])
        qk = sb("qk", [P, 2, L])
        rest = sb("rest", [P, 2, L])
        parts = sb("parts", [P, 2, 2, 3, L], BF16)
        neg_max = sb("neg_max", [P, 2, UNITS * HU])
        exp_sum = sb("exp_sum", [P, 2, LT * H])
        att = sb("att", [P, 2, LT * H])
        mod_b = [sb(f"mod_b{p}", [P, MODROWS, D]) for p in range(2)]
        w_gated = sb("w_gated", [P, D])
        x_bias = sb("x_bias", [P, LT, D])
        opt = sb("opt", [P, LT, D])
        opt_t = sb("opt_t", [P, L])
        bn2 = sb("bn2", [P, LT, 6])
        mv2 = sb("mv2", [P, LT, 2])
        rstd2 = sb("rstd2", [P, 2, LT])
        xhat2 = sb("xhat2", [P, LT, D])
        h_scaled = sb("h_scaled", [P, LT, D])
        h2_t = sb("h2_t", [P, L])
        rows = [sb(f"rows{p}", [P, LT, ROW]) for p in range(2)]
        logit = sb("logit", [P, LT, E])
        top = sb("top", [P, LT])
        below = sb("below", [P, LT, E])
        exp_l = sb("exp_l", [P, LT, E])
        is_top = sb("is_top", [P, LT, E])
        rank_top = sb("rank_top", [P, LT])
        one_hot = sb("one_hot", [P, LT, E])
        one_hot_b = sb("one_hot_b", [P, LT, E], BF16)
        weight = sb("weight", [P, 2, LT])
        place = sb("place", [P, 2, LT, E])
        place_f = sb("place_f", [P, LT])
        place_i = [sb(f"place_i{p}", [P, LT], I32) for p in range(2)]
        next_row = sb("next_row", [P, E])
        token_id = sb("token_id", [P, LT], I32)
        count_f = sb("count_f", [P, 8, E])
        count_i = sb("count_i", [P, 2, E], I32)
        tile_no = sb("tile_no", [1, NT])
        x_room = x_s[:, :, :].rearrange("p t d -> p (t d)")

        def reuse(offset, *shape):
            size = shape[0] if len(shape) == 1 else shape[0] * shape[1]
            part = x_room[:, offset:offset + size]
            return part if len(shape) == 1 else part.rearrange("p (a b) -> p a b", b=shape[1])

        map_a, map_b, map_c = (reuse(n * NT * E, NT, E)[0:1] for n in range(3))
        map_f = sb("map_f", [1, 4, NT])
        tile_expert = sb("tile_expert", [1, NT], I32)
        tile_row = sb("tile_row", [1, NT], I32)
        end_row = sb("end_row", [1, E], I32)
        rows_at = 3 * NT * E
        rows_in = [reuse(rows_at + s * ROW, ROW) for s in range(SLOTS)]
        x_t = sb("x_t", [P, 2, P])
        w1_e = sb("w1_e", [P, 2, W1X])
        hid = sb("hid", [P, 2, FH, P])
        y_s = sb("y_s", [P, 2, D])
        out_s = [reuse(rows_at + SLOTS * ROW + s * D, D) for s in range(SLOTS)]

        scores = ps("scores", [P, RING, HU * L])
        side_a = ps("side_a", [P, 512])
        side_b = ps("side_b", [P, 512])
        xhat_v = side_a[:, 0:L]
        opt_pr = side_a[:, L:2 * L]
        h2_turn = side_b[:, 0:L]
        logit_p = side_b[:, L:L + LT * E]
        rank_p = side_b[:, L + 32:L + 32 + LT * E]
        total_p = side_b[:, L + 64:L + 64 + E]
        hidden = [scores[:, 0, m * 512:m * 512 + F] for m in range(2)]
        expert_out = [scores[:, 1, m * 512:m * 512 + D] for m in range(2)]
        turned = [scores[:, 2, m * 512:m * 512 + P] for m in range(2)]

        w_in_loaded = sem("w_in_loaded")
        w_moe_loaded = sem("w_moe_loaded")
        x_loaded = [sem(f"x_loaded{n}") for n in range(len(X_CHUNKS))]
        consts_set = sem("consts_set")
        exp_c = sem("exp_c")
        silu_done = sem("silu_done")
        mod_done = sem("mod_done")
        mod_ready = sem("mod_ready")
        mod_stored = sem("mod_stored")
        mod_b_loaded = [sem("mod_b_loaded0"), sem("mod_b_loaded1")]
        pad_set = sem("pad_set")
        pad_stored = sem("pad_stored")
        dve_steps = sem("dve_steps")
        pool_steps = sem("pool_steps")
        dve_held = sem("dve_held")
        sp_held = sem("sp_held")
        pool_held = sem("pool_held")
        stats1 = sem("stats1")
        xhat1_ready = sem("xhat1_ready")
        xhat1_turned = sem("xhat1_turned")
        h_ready = sem("h_ready")
        qk_done = sem("qk_done")
        v_done = sem("v_done")
        qk_ready = sem("qk_ready")
        v_ready = sem("v_ready")
        parts_ready = sem("parts_ready")
        parts_stored = sem("parts_stored")
        stacked = [sem("stacked0"), sem("stacked1")]
        scored = sem("scored")
        maxed = sem("maxed")
        exped = sem("exped")
        att_ready = sem("att_ready")
        gated = sem("gated")
        opt_ready = sem("opt_ready")
        opt_turned = sem("opt_turned")
        opt_t_ready = sem("opt_t_ready")
        projected = sem("projected")
        stats2 = sem("stats2")
        h2_ready = sem("h2_ready")
        h2_turned = sem("h2_turned")
        h2_t_ready = sem("h2_t_ready")
        logits_done = sem("logits_done")
        below_ready = sem("below_ready")
        expl_ready = sem("expl_ready")
        hot_ready = sem("hot_ready")
        ranked = sem("ranked")
        placed = sem("placed")
        weighted = sem("weighted")
        scattered = [sem("scattered0"), sem("scattered1")]
        map_ready = sem("map_ready")
        tails_padded = sem("tails_padded")
        tails_padded2 = sem("tails_padded2")
        rows_loaded = [sem(f"rows_loaded{s}") for s in range(SLOTS)]
        x_turned = sem("x_turned")
        x_t_ready = sem("x_t_ready")
        w1_ready = sem("w1_ready")
        hid_done = sem("hid_done")
        hid_ready = sem("hid_ready")
        y_done = sem("y_done")
        out_ready = sem("out_ready")
        out_stored = [sem(f"out_stored{s}") for s in range(SLOTS)]

        LOADS_IN = 14
        SETS = 8

        block = ctx.enter_context(nc.Block())

        @block.sync
        def _(sp):
            steps = Steps(sp, sp_held, sp_held)
            sp.dma_start(c_s[:, :], c_t).then_inc(w_in_loaded, 16)
            sp.dma_start(wmod_s[:, :], wmod).then_inc(w_in_loaded, 16)

            def load_x(n):
                t = slice(LT * X_CHUNKS[n][0], LT * X_CHUNKS[n][1])
                sp.dma_start(x_s[:, t, :], x_tiles[:, t, :]).then_inc(x_loaded[n], 16)

            load_x(0)
            load_x(1)
            sp.dma_start(ident_s[:, :], ident).then_inc(w_in_loaded, 16)
            sp.dma_start(w_qkv_s[:, :, :], w_qkv).then_inc(w_in_loaded, 16)
            sp.dma_start(b_qk_s[:, :], b_qk).then_inc(w_in_loaded, 16)
            sp.dma_start(b_v_s[:, :], b_v.broadcast_to([P, D])).then_inc(w_in_loaded, 16)
            sp.dma_start(w_out_s[:, :], w_out).then_inc(w_in_loaded, 16)
            sp.dma_start(b_out_s[:, :], b_out.broadcast_to([B, D])).then_inc(w_in_loaded, 16)
            sp.dma_start(router_s[:, :], router_w).then_inc(w_in_loaded, 16)
            sp.dma_start(before_f[:, :], before).then_inc(w_in_loaded, 16)
            sp.dma_start(expert_s[:, :, :], expert_row.broadcast_to([P, 3 * E])).then_inc(w_in_loaded, 16)
            sp.dma_start(tile_no[:, :], tile_numbers).then_inc(w_in_loaded, 16)
            sp.dma_start(token_id[:, :], token_numbers).then_inc(w_in_loaded, 16)
            sp.dma_start(next_row[:, :], first_row.broadcast_to([P, E])).then_inc(w_in_loaded, 16)
            load_x(2)
            load_x(3)
            sp.wait_ge(pad_set, 2)
            sp.dma_start(table[PAD_AT:PAD_AT + P, :], pad_tile[:, :]).then_inc(pad_stored, 16)
            sp.wait_ge(mod_ready, 1)
            sp.dma_start(mod_rows, rows_out[:, :, :].rearrange("b r d -> b (r d)")).then_inc(mod_stored, 16)

            def store_parts(b, p):
                sp.wait_ge(parts_ready, b + 1)
                sp.dma_start(parts_dram[p].rearrange("q s r t -> r (q s) t"),
                             parts[:, p].rearrange("r q s t -> r (q s) t")).then_inc(parts_stored, 16)
                sp.wait_ge(parts_stored, 16 * b + 16)
                steps.plain()

            def load_stacks(b, p):
                for n, (qp, kp) in enumerate(zip(Q_PART, K_PART)):
                    r = slice(DH * n, DH * n + DH)
                    sp.dma_start(q_stack[p][r, :, :], parts_dram[p, 0, qp].rearrange("(h d) t -> d h t", d=DH)).then_inc(stacked[p], 16)
                    sp.dma_start(k_stack[p][r, :, :], parts_dram[p, 1, kp].rearrange("(h d) t -> d h t", d=DH)).then_inc(stacked[p], 16)

            sp.wait_ge(consts_set, SETS)
            for b in range(2):
                store_parts(b, b)
                load_stacks(b, b)
            sp.wait_ge(mod_stored, 16)
            sp.dma_start(w1x_s[:, :, :], w1x).then_inc(w_moe_loaded, 16)
            sp.dma_start(w2_s[:, :, :, :], w2).then_inc(w_moe_loaded, 16)
            sp.dma_start(b2_s[:, :, :], b2.broadcast_to([P, E * D])).then_inc(w_moe_loaded, 16)

            def iteration(b, p):
                if has_prep(b):
                    store_parts(b + 2, p)
                need(sp, weighted, b - 1)
                sp.dma_start(mod_b[p][:, :, :], mod_rows[ds(b, 1), :].broadcast_to([P, MODROWS * D])).then_inc(mod_b_loaded[p], 16)
                if has_prep(b):
                    sp.wait_ge(scored, UNITS * b + UNITS)
                    load_stacks(b + 2, p)

            over_batches(sp, iteration, lambda b, p: None)

            sp.wait_ge(scattered[0], 16 * T // 2)
            sp.wait_ge(scattered[1], 16 * T // 2)
            sp.wait_ge(map_ready, 1)
            for e in range(0, E):
                at = sp.value_load(end_row[0:1, e:e + 1], min_val=e * ROOM, max_val=e * ROOM + NTOK)
                sp.dma_start(table[ds(at, P), :], pad_tile[:, :]).then_inc(tails_padded, 16)
            sp.wait_ge(tails_padded, 16 * E)
            sp.wait_ge(pad_stored, 16)

            def load(j, s, turn):
                at = sp.value_load(tile_row[0:1, ds(j, 1)], min_val=0, max_val=PAD_AT)
                need(sp, out_stored[s], 16 * turn)
                sp.dma_start(rows_in[s][:, :], table[ds(at, P), :]).then_inc(rows_loaded[s], 16)

            over_tiles(sp, load, 0)
            for s in range(SLOTS):
                sp.wait_ge(out_stored[s], 16 * NT // SLOTS)

        @block.gpsimd
        def _(pool):
            steps = Steps(pool, pool_steps, pool_held)
            pool.memset(ones_s[:, :], 1.0).then_inc(consts_set, 1)
            for p in range(2):
                pool.memset(q_stack[p][:, :, :], 0.0).then_inc(consts_set, 1)
                pool.memset(k_stack[p][:, :, :], 0.0).then_inc(consts_set, 1)
            pool.memset(minus_half[:, :], -0.5).then_inc(consts_set, 1)
            pool.memset(eps_s[:, :], EPS).then_inc(consts_set, 1)
            pool.memset(batch_s[:, :], L).then_inc(consts_set, 1)
            pool.memset(pad_tile[:, 0:ID], 0.0).then_inc(pad_set, 1)
            pool.memset(pad_tile[:, ID:ROW].bitcast(I32), int(NO_TOKEN)).then_inc(pad_set, 1)
            pool.wait_ge(consts_set, SETS)

            def normalise(mv, rstd, centred, src, dst):
                def by_token(v):
                    return v.rearrange("p (t o) -> p t o", o=1).broadcast_to([P, LT, D])

                pool.tensor_tensor(centred[:, :, :], src, mv[:, :, 0:1].broadcast_to([P, LT, D]), ALU.subtract)
                steps.then(pool.tensor_tensor(rstd[:, 0, :], mv[:, :, 1], eps_s[:, :], ALU.add))
                steps.then(pool.tensor_tensor(rstd[:, 1, :], rstd[:, 0, :], minus_half[:, :], ALU.pow))
                return pool.tensor_tensor(dst[:, :, :], centred[:, :, :], by_token(rstd[:, 1, :]), ALU.mult)

            def norm_x(b):
                pool.wait_ge(stats1, b + 1)
                need(pool, xhat1_ready, b)
                need(pool, xhat1_turned, b)
                normalise(mv1, rstd1, centred1, x_s[:, ds(LT * b, LT), :], xhat1).then_inc(xhat1_ready, 1)

            def split(b, p):
                pool.wait_ge(qk_ready, b + 1)
                need(pool, parts_stored, 16 * b - 16)
                steps.plain()
                steps.then(pool.tensor_scalar(parts[:, p, :, 0, :], qk[:, :, :], 1.0, None, ALU.mult))
                steps.then(pool.tensor_tensor(rest[:, :, :], qk[:, :, :], parts[:, p, :, 0, :], ALU.subtract), plain=True)
                steps.then(pool.tensor_scalar(parts[:, p, :, 1, :], rest[:, :, :], 1.0, None, ALU.mult))
                pool.tensor_tensor(parts[:, p, :, 2, :], rest[:, :, :], parts[:, p, :, 1, :], ALU.subtract).then_inc(parts_ready, 1)

            def gate(b, p):
                pool.wait_ge(mod_b_loaded[p], 8 * (b - p) + 16)
                need(pool, stats2, b)
                pool.tensor_tensor(w_gated[:, :], w_out_s[:, :], mod_b[p][:, 0, :], ALU.mult)
                pool.tensor_tensor(x_bias[:, :, :], x_s[:, ds(LT * b, LT), :],
                                   mod_b[p][:, 1:2, :].broadcast_to([P, LT, D]), ALU.add).then_inc(gated, 1)

            def attend(b, p):
                pool.wait_ge(att_ready, b + 1)
                need(pool, opt_turned, b)
                for t in range(LT):
                    last = pool.tensor_tensor(
                        opt[:, t, :].rearrange("p (h d) -> p h d", d=DH),
                        v_s[:, ds(LT * b + t, 1), :].rearrange("p t (h d) -> p (t h) d", d=DH),
                        att[:, 1, t * H:t * H + H].rearrange("p (h o) -> p h o", o=1).broadcast_to([P, H, DH]),
                        ALU.mult)
                last.then_inc(opt_ready, 1)

            def norm_x2(b, p):
                pool.wait_ge(stats2, b + 1)
                need(pool, scattered[p], 8 * LT * (b - p))
                steps.then(normalise(mv2, rstd2, centred2, rows[p][:, :, X2:X2 + D], xhat2))
                steps.then(pool.tensor_tensor(h_scaled[:, :, :], xhat2[:, :, :],
                                              mod_b[p][:, 2:3, :].broadcast_to([P, LT, D]), ALU.mult))
                pool.tensor_tensor(rows[p][:, :, H2:H2 + D], h_scaled[:, :, :],
                                   mod_b[p][:, 3:4, :].broadcast_to([P, LT, D]), ALU.add).then_inc(h2_ready, 1)

            def scatter(b, p):
                pool.wait_ge(placed, b + 1)
                pool.tensor_tensor(rows[p][:, :, ID:ROW].bitcast(I32), token_id[:, :].rearrange("p (t o) -> p t o", o=1),
                                   batch_s[:, :].rearrange("p (t o) -> p t o", o=1), ALU.add)
                steps.then(pool.tensor_tensor(token_id[:, :], token_id[:, :], batch_s[:, :], ALU.add), plain=True)
                for t in range(LT):
                    last = pool.tensor_scalar(rows[p][:, t, GW:GW + D], mod_b[p][:, 4, :], weight[:, 1, t:t + 1], None, ALU.mult)
                last.then_inc(weighted, 1)
                pool.wait_ge(weighted, b + 1)
                steps.plain()
                for t in range(LT):
                    pool.indirect_dma_start(table, bass.IndirectOffsetOnAxis(ap=place_i[p][:, t:t + 1], axis=0),
                                            rows[p][:, t, :], None).then_inc(scattered[p], 16)

            pool.wait_ge(w_in_loaded, 16 * LOADS_IN)
            for b in range(2):
                norm_x(b)
                split(b, b)
            norm_x(2)

            def iteration(b, p):
                if has_tail(b):
                    gate(b - 1, 1 - p)
                    attend(b - 1, 1 - p)
                if has_norm(b):
                    norm_x(b + 3)
                if has_routing(b):
                    scatter(b - 2, p)
                if has_tail(b):
                    norm_x2(b - 1, 1 - p)
                if has_prep(b):
                    split(b + 2, p)

            def drain(b, p):
                gate(b - 1, 1 - p)
                attend(b - 1, 1 - p)
                scatter(b - 2, p)
                norm_x2(b - 1, 1 - p)
                scatter(b - 1, 1 - p)

            over_batches(pool, iteration, drain, steps, 2 * STEPS_POOL)

            def store(j, s, turn):
                pool.wait_ge(out_ready, j + 1)
                steps.plain()
                pool.indirect_dma_start(out_rows, bass.IndirectOffsetOnAxis(ap=rows_in[s][:, ID:ROW].bitcast(I32), axis=0),
                                        out_s[s][:, :], None, bounds_check=NTOK - 1, oob_is_err=False).then_inc(out_stored[s], 16)

            over_tiles(pool, store, 0)

        @block.scalar
        def _(act):
            act.wait_ge(w_in_loaded, 16 * LOADS_IN)
            act.activation(silu_s[:, 0, :], c_s[:, :], ACT.Exp, scale=-1.0).then_inc(exp_c, 1)

            def iteration(b, p):
                for u in range(UNITS):
                    act.wait_ge(maxed, UNITS * b + u + 1)
                    buf = scores[:, BUF_OF[u], :]
                    for k in range(HU):
                        n = u * HU + k
                        last = act.activation(buf[:, k * L:k * L + L], buf[:, k * L:k * L + L], ACT.Exp,
                                              bias=neg_max[:, p, n:n + 1], accum_out=exp_sum[:, p, n:n + 1])
                    last.then_inc(exped, 1)
                    if u == 3 and has_routing(b):
                        router_exp(b - 2)

            def router_exp(b):
                act.wait_ge(below_ready, b + 1)
                act.activation(exp_l[:, :, :], below[:, :, :], ACT.Exp).then_inc(expl_ready, 1)

            def drain(b, p):
                router_exp(b - 2)
                router_exp(b - 1)

            over_batches(act, iteration, drain)

            def gelu(j, s, turn):
                if isinstance(j, int) and j < 1:
                    return
                m = (s - 1) % 2
                act.wait_ge(hid_done, j)
                need(act, y_done, j - 2)
                for f in range(FH):
                    last = act.activation(hid[:, m, f, :], hidden[m][:, f * P:f * P + P], ACT.Gelu,
                                          bias=w1_e[:, m, F + f:F + f + 1])
                last.then_inc(hid_ready, 1)

            over_tiles(act, gelu, 1)

        @block.tensor
        def _(pe):
            pe.wait_ge(silu_done, 1)
            pe.wait_ge(w_in_loaded, 16 * LOADS_IN)
            silu = silu_s[:, 2, :]
            for n in range(2):
                pe.matmul(scores[0:B, 0, n * 512:n * 512 + 3 * D], silu, wmod_s[:, n * 3 * D:(n + 1) * 3 * D], start=True, stop=True)
            for n in range(2):
                last = pe.matmul(scores[:, 1, n * 512:n * 512 + B], wmod_s[:, n * D:n * D + D], silu, start=True, stop=True)
            last.then_inc(mod_done, 1)

            def turn_x(b):
                pe.wait_ge(xhat1_ready, b + 1)
                need(pe, v_ready, b)
                need(pe, stats2, b - 3)
                for t in range(LT):
                    last = pe.transpose(xhat_v[:, t * P:t * P + P], xhat1[:, t, :], ident_s[:, :])
                last.then_inc(xhat1_turned, 1)

            def project_v(b):
                pe.wait_ge(h_ready, b + 1)
                for t in range(LT):
                    last = pe.matmul(xhat_v[:, t * P:t * P + P], h_t[:, t * P:t * P + P], w_qkv_s[:, 2, :], start=True, stop=True)
                last.then_inc(v_done, 1)

            def project_qk(b):
                need(pe, placed, b - 3)
                need(pe, qk_ready, b)
                for n in range(2):
                    last = pe.matmul(side_b[:, n * L:n * L + L], w_qkv_s[:, n, :], h_t[:, :], start=True, stop=True)
                last.then_inc(qk_done, 1)

            def score(b, p, u):
                if u == 0:
                    pe.wait_ge(stacked[p], (2 * 16 * COMBOS // 2) * (b - p) + 2 * 16 * COMBOS)
                need(pe, exped, UNITS * b + u - BACK[u] + 1)
                t, g = u // (H // HU), u % (H // HU)
                for k in range(HU):
                    h = HU * g + k
                    last = pe.matmul(scores[:, BUF_OF[u], k * L:k * L + L], q_stack[p][:, h, t * P:t * P + P],
                                     k_stack[p][:, h, :], start=True, stop=True)
                last.then_inc(scored, 1)

            def turn_opt(b, ahead):
                pe.wait_ge(opt_ready, b + 1)
                need(pe, stats2, b)
                pe.wait_ge(v_ready, ahead)
                for t in range(LT):
                    last = pe.transpose(opt_pr[:, t * P:t * P + P], opt[:, t, :], ident_s[:, :])
                last.then_inc(opt_turned, 1)

            def project_out(b):
                pe.wait_ge(opt_t_ready, b + 1)
                pe.wait_ge(gated, b + 1)
                for t in range(LT):
                    last = pe.matmul(opt_pr[:, t * P:t * P + P], opt_t[:, t * P:t * P + P], w_gated[:, :], start=True, stop=True)
                last.then_inc(projected, 1)

            def turn_h2(b, p, ahead):
                pe.wait_ge(h2_ready, b + 1)
                need(pe, placed, b)
                pe.wait_ge(qk_ready, ahead)
                for t in range(LT):
                    last = pe.transpose(h2_turn[:, t * P:t * P + P], rows[p][:, t, H2:H2 + D], ident_s[:, :])
                last.then_inc(h2_turned, 1)

            def route(b):
                pe.wait_ge(h2_t_ready, b + 1)
                for t in range(LT):
                    last = pe.matmul(logit_p[:, t * E:t * E + E], h2_t[:, t * P:t * P + P], router_s[:, :], start=True, stop=True)
                last.then_inc(logits_done, 1)

            def rank(b):
                pe.wait_ge(hot_ready, b + 1)
                pe.matmul(rank_p[:, 0:E], before_s[:, :], one_hot_b[:, 0, :], start=True, stop=True)
                pe.matmul(rank_p[:, E:2 * E], before_s[:, :], one_hot_b[:, 1, :], start=True, stop=False)
                pe.matmul(rank_p[:, E:2 * E], ones_s[:, :], one_hot_b[:, 0, :], start=False, stop=True)
                pe.matmul(total_p, ones_s[:, :], one_hot_b[:, 0, :], start=True, stop=False)
                pe.matmul(total_p, ones_s[:, :], one_hot_b[:, 1, :], start=False, stop=True).then_inc(ranked, 1)

            pe.wait_ge(w_in_loaded, 16 * LOADS_IN)
            pe.wait_ge(mod_ready, 1)
            for b in range(2):
                turn_x(b)
                project_v(b)
                project_qk(b)

            def up_to(b):
                return min(b, B) if isinstance(b, int) else b

            def iteration(b, p):
                score(b, p, 0)
                if has_prep(b):
                    turn_x(b + 2)
                if has_routing(b):
                    turn_h2(b - 2, p, up_to(b + 2))
                score(b, p, 1)
                if has_routing(b):
                    route(b - 2)
                score(b, p, 2)
                if has_prep(b):
                    project_v(b + 2)
                score(b, p, 3)
                if has_routing(b):
                    rank(b - 2)
                if has_tail(b):
                    turn_opt(b - 1, up_to(b + 3))
                score(b, p, 4)
                if has_prep(b):
                    project_qk(b + 2)
                if has_tail(b):
                    project_out(b - 1)
                score(b, p, 5)
                score(b, p, 6)
                score(b, p, 7)

            def drain(b, p):
                turn_h2(b - 2, p, B)
                route(b - 2)
                rank(b - 2)
                turn_opt(b - 1, B)
                project_out(b - 1)
                turn_h2(b - 1, 1 - p, B)
                route(b - 1)
                rank(b - 1)

            over_batches(pe, iteration, drain)

            pe.wait_ge(map_ready, 1)
            pe.wait_ge(w_moe_loaded, 48)

            def tile(j, s, turn):
                static = isinstance(j, int)
                if not (static and j >= NT):
                    pe.wait_ge(rows_loaded[s], 16 * turn + 16)
                    need(pe, x_t_ready, j - 1)
                    pe.transpose(turned[s % 2], rows_in[s][:, H2:H2 + D], ident_s[:, :]).then_inc(x_turned, 1)
                if not (static and not 0 <= j - 1 < NT):
                    m = (s - 1) % 2
                    pe.wait_ge(x_t_ready, j)
                    pe.wait_ge(w1_ready, j)
                    need(pe, hid_ready, j - 2)
                    for f in range(FH):
                        last = pe.matmul(hidden[m][:, f * P:f * P + P], w1_e[:, m, f * P:f * P + P], x_t[:, m, :], start=True, stop=True)
                    last.then_inc(hid_done, 1)
                if not (static and not 0 <= j - 2 < NT):
                    m = s % 2
                    e = pe.value_load(tile_expert[0:1, ds(j - 2, 1)], min_val=0, max_val=E - 1)
                    pe.wait_ge(hid_ready, j - 1)
                    need(pe, out_ready, j - 3)
                    for f in range(FH):
                        last = pe.matmul(expert_out[m], hid[:, m, f, :], w2_s[:, ds(e, 1), f, :], start=(f == 0), stop=(f == FH - 1))
                    last.then_inc(y_done, 1)

            over_tiles(pe, tile, 2)

        @block.vector
        def _(dve):
            steps = Steps(dve, dve_steps, dve_held)
            dve.wait_ge(exp_c, 1)
            steps.then(dve.tensor_scalar(silu_s[:, 0, :], silu_s[:, 0, :], 1.0, None, ALU.add))
            steps.then(dve.reciprocal(silu_s[:, 1, :], silu_s[:, 0, :]))
            dve.tensor_tensor(silu_s[:, 2, :], c_s[:, :], silu_s[:, 1, :], ALU.mult).then_inc(silu_done, 1)
            dve.wait_ge(w_in_loaded, 16 * LOADS_IN)
            dve.tensor_copy(before_s[:, :], before_f[:, :])
            dve.tensor_scalar(w_qkv_s[:, 0, :], w_qkv_s[:, 0, :], SCALE, None, ALU.mult)
            dve.tensor_scalar(b_qk_s[:, 0:1], b_qk_s[:, 0:1], SCALE, None, ALU.mult)
            dve.wait_ge(mod_done, 1)
            for n in range(2):
                dve.tensor_copy(mod_s[:, n * 3 * D:(n + 1) * 3 * D], scores[0:B, 0, n * 512:n * 512 + 3 * D])
            dve.tensor_copy(shift_a[:, :], scores[:, 1, 0:B])
            steps.then(dve.tensor_scalar(scale_a[:, :], scores[:, 1, 512:512 + B], 1.0, None, ALU.add))
            for n, chunk in enumerate((2, 5)):
                g = mod_s[:, chunk * D:chunk * D + D]
                w = slice(n * D, n * D + D)
                steps.then(dve.tensor_scalar(mod_tmp[:, 0, w], g, 0.0, 2.0, ALU.is_ge, ALU.mult))
                steps.then(dve.tensor_scalar(mod_tmp[:, 1, w], g, -1.0, None, ALU.mult))
                steps.then(dve.tensor_tensor(mod_tmp[:, 2, w], mod_tmp[:, 1, w], g, ALU.max))
                steps.then(dve.tensor_scalar(mod_tmp[:, 1, w], mod_tmp[:, 2, w], 0.25, None, ALU.max))
                steps.then(dve.tensor_scalar(mod_tmp[:, 2, w], mod_tmp[:, 0, w], -1.0, None, ALU.add))
                steps.then(dve.tensor_tensor(rows_out[:, (0, 4)[n], :], mod_tmp[:, 1, w], mod_tmp[:, 2, w], ALU.mult))
            dve.tensor_tensor(rows_out[:, 1, :], rows_out[:, 0, :], b_out_s[:, :], ALU.mult)
            dve.tensor_scalar(rows_out[:, 2, :], mod_s[:, 4 * D:5 * D], 1.0, None, ALU.add)
            dve.tensor_copy(rows_out[:, 3, :], mod_s[:, 3 * D:4 * D]).then_inc(mod_ready, 1)

            def stats(src, bn, mv):
                for t in range(LT):
                    ins = dve.bn_stats(bn[:, t, :], src(t))
                steps.then(ins, plain=True)
                for t in range(LT):
                    last = dve.bn_aggr(mv[:, t, :], bn[:, t, :])
                return last

            def stats_x(b, p):
                if isinstance(b, int):
                    dve.wait_ge(x_loaded[next(n for n, c in enumerate(X_CHUNKS) if c[0] <= b < c[1])], 16)
                need(dve, xhat1_ready, b)
                stats(lambda t: x_s[:, ds(LT * b + t, 1), :].rearrange("p t d -> p (t d)"), bn1, mv1).then_inc(stats1, 1)

            def make_h(b):
                dve.wait_ge(xhat1_turned, b + 1)
                dve.tensor_scalar(h_t[:, :], xhat_v, scale_a[:, ds(b, 1)], shift_a[:, ds(b, 1)], ALU.mult, ALU.add).then_inc(h_ready, 1)

            def take_qk(b):
                dve.wait_ge(qk_done, b + 1)
                need(dve, parts_ready, b)
                dve.tensor_tensor(qk[:, :, :], side_b[:, :].rearrange("p (s t) -> p s t", s=2),
                                  b_qk_s[:, :].rearrange("p (s o) -> p s o", o=1).broadcast_to([P, 2, L]), ALU.add).then_inc(qk_ready, 1)

            def take_v(b):
                dve.wait_ge(v_done, b + 1)
                dve.tensor_tensor(v_s[:, ds(LT * b, LT), :], xhat_v.rearrange("p (t d) -> p t d", t=LT),
                                  b_v_s[:, :].rearrange("p (o d) -> p o d", o=1).broadcast_to([P, LT, D]), ALU.add).then_inc(v_ready, 1)

            def row_max(b, p, u):
                dve.wait_ge(scored, UNITS * b + u + 1)
                dve.tensor_reduce(neg_max[:, p, u * HU:u * HU + HU], scores[:, BUF_OF[u], :].rearrange("p (h m) -> p h m", h=HU),
                                  AX_X, ALU.max, negate=True).then_inc(maxed, 1)

            def attention_sums(b, p):
                dve.wait_ge(exped, UNITS * b + UNITS)
                need(dve, opt_ready, b)
                steps.then(dve.reciprocal(att[:, 0, :], exp_sum[:, p, :]))
                dve.tensor_tensor(att[:, 1, :], exp_sum[:, p, :], att[:, 0, :], ALU.mult).then_inc(att_ready, 1)

            def take_opt(b):
                dve.wait_ge(opt_turned, b + 1)
                dve.tensor_copy(opt_t[:, :], opt_pr).then_inc(opt_t_ready, 1)

            def residual(b, p):
                dve.wait_ge(projected, b + 1)
                need(dve, scattered[p], 8 * LT * (b - p))
                steps.then(dve.tensor_tensor(rows[p][:, :, X2:X2 + D], opt_pr.rearrange("p (t d) -> p t d", t=LT), x_bias[:, :, :], ALU.add))
                need(dve, h2_ready, b)
                stats(lambda t: rows[p][:, t, X2:X2 + D], bn2, mv2).then_inc(stats2, 1)

            def take_h2(b):
                dve.wait_ge(h2_turned, b + 1)
                dve.tensor_copy(h2_t[:, :], h2_turn).then_inc(h2_t_ready, 1)

            def bcast(v):
                return v.rearrange("p (t o) -> p t o", o=1).broadcast_to([P, LT, E])

            def per_tile(v):
                return v.rearrange("p (o e) -> p o e", o=1).broadcast_to([P, LT, E])

            def choose(b):
                dve.wait_ge(logits_done, b + 1)
                steps.then(dve.tensor_copy(logit[:, :, :], logit_p.rearrange("p (t e) -> p t e", t=LT)))
                steps.then(dve.tensor_reduce(top[:, :], logit[:, :, :], AX_X, ALU.max))
                dve.tensor_tensor(below[:, :, :], logit[:, :, :], bcast(top[:, :]), ALU.subtract).then_inc(below_ready, 1)
                steps.then(dve.tensor_tensor(is_top[:, :, :], logit[:, :, :], bcast(top[:, :]), ALU.is_equal))
                steps.then(dve.tensor_tensor(place[:, 0], is_top[:, :, :], per_tile(expert_s[:, 0, :]), ALU.mult))
                steps.then(dve.tensor_reduce(rank_top[:, :], place[:, 0], AX_X, ALU.max))
                steps.then(dve.tensor_tensor(one_hot[:, :, :], place[:, 0], bcast(rank_top[:, :]), ALU.is_equal))
                dve.tensor_copy(one_hot_b[:, :, :], one_hot[:, :, :]).then_inc(hot_ready, 1)

            def find_place(b, p):
                dve.wait_ge(expl_ready, b + 1)
                steps.then(dve.tensor_reduce(weight[:, 0, :], exp_l[:, :, :], AX_X, ALU.add))
                need(dve, weighted, b)
                dve.reciprocal(weight[:, 1, :], weight[:, 0, :])
                dve.wait_ge(ranked, b + 1)
                steps.then(dve.tensor_tensor(place[:, 0], rank_p.rearrange("p (t e) -> p t e", t=LT), per_tile(next_row[:, :]), ALU.add))
                steps.then(dve.tensor_tensor(place[:, 1], place[:, 0], one_hot[:, :, :], ALU.mult))
                steps.then(dve.tensor_reduce(place_f[:, :], place[:, 1], AX_X, ALU.add))
                dve.tensor_tensor(next_row[:, :], next_row[:, :], total_p, ALU.add)
                dve.tensor_copy(place_i[p][:, :], place_f[:, :]).then_inc(placed, 1)

            for b in range(2):
                stats_x(b, b)
                make_h(b)
                take_v(b)
                take_qk(b)
            stats_x(2, 0)

            def iteration(b, p):
                row_max(b, p, 0)
                if has_prep(b):
                    make_h(b + 2)
                row_max(b, p, 1)
                if has_tail(b):
                    attention_sums(b - 1, 1 - p)
                if has_routing(b):
                    take_h2(b - 2)
                row_max(b, p, 2)
                if has_routing(b):
                    choose(b - 2)
                row_max(b, p, 3)
                if has_prep(b):
                    take_v(b + 2)
                if has_norm(b):
                    stats_x(b + 3, 1 - p)
                row_max(b, p, 4)
                if has_routing(b):
                    find_place(b - 2, p)
                if has_tail(b):
                    take_opt(b - 1)
                row_max(b, p, 5)
                if has_prep(b):
                    take_qk(b + 2)
                if has_tail(b):
                    residual(b - 1, 1 - p)
                row_max(b, p, 6)
                row_max(b, p, 7)

            def drain(b, p):
                attention_sums(b - 1, 1 - p)
                take_h2(b - 2)
                choose(b - 2)
                find_place(b - 2, p)
                take_opt(b - 1)
                residual(b - 1, 1 - p)
                take_h2(b - 1)
                choose(b - 1)
                find_place(b - 1, 1 - p)

            over_batches(dve, iteration, drain, steps, 2 * STEPS_DVE, lambda: dve.wait_ge(x_loaded[3], 16))

            first_e = expert_s[:, 2, :]
            dve.wait_ge(placed, B)
            steps.then(dve.tensor_tensor(count_f[:, 0, :], next_row[:, :], first_e, ALU.subtract))
            steps.then(dve.tensor_scalar(count_f[:, 1, :], count_f[:, 0, :], float(P - 1), None, ALU.add))
            steps.then(dve.tensor_copy(count_i[:, 0, :], count_f[:, 1, :]))
            steps.then(dve.tensor_scalar(count_i[:, 1, :], count_i[:, 0, :], P.bit_length() - 1, None, ALU.arith_shift_right))
            steps.then(dve.tensor_copy(count_f[:, 2, :], count_i[:, 1, :]))
            at, shift = 2, 1
            while shift < E:
                to = {2: 3, 3: 4, 4: 3}[at]
                dve.tensor_copy(count_f[:, to, 0:shift], count_f[:, at, 0:shift])
                steps.then(dve.tensor_tensor(count_f[:, to, shift:E], count_f[:, at, shift:E], count_f[:, at, 0:E - shift], ALU.add))
                at, shift = to, 2 * shift
            upto = count_f[0:1, at, :]
            steps.then(dve.tensor_tensor(count_f[:, 5, :], count_f[:, at, :], count_f[:, 2, :], ALU.subtract))
            from_ = count_f[0:1, 5, :]
            steps.then(dve.tensor_scalar(count_f[:, 6, :], count_f[:, 5, :], -float(P), None, ALU.mult))
            steps.then(dve.tensor_tensor(count_f[:, 7, :], count_f[:, 6, :], first_e, ALU.add))
            dve.tensor_copy(end_row[:, :], next_row[0:1, :])
            tiles = tile_no[:, :].rearrange("p (j o) -> p j o", o=1).broadcast_to([1, NT, E])

            def experts(v):
                return v.rearrange("p (o e) -> p o e", o=1).broadcast_to([1, NT, E])

            dve.tensor_tensor(map_a[:, :, :], tiles, experts(from_), ALU.is_ge)
            steps.then(dve.tensor_tensor(map_b[:, :, :], tiles, experts(upto), ALU.is_ge))
            steps.then(dve.tensor_tensor(map_c[:, :, :], map_a[:, :, :], map_b[:, :, :], ALU.subtract))
            dve.tensor_reduce(map_f[:, 0, :], map_c[:, :, :], AX_X, ALU.add)
            steps.then(dve.tensor_tensor(map_a[:, :, :], map_c[:, :, :], experts(expert_s[0:1, 1, :]), ALU.mult))
            steps.then(dve.tensor_reduce(map_f[:, 1, :], map_a[:, :, :], AX_X, ALU.add))
            dve.tensor_copy(tile_expert[:, :], map_f[:, 1, :])
            steps.then(dve.tensor_tensor(map_b[:, :, :], map_c[:, :, :], experts(count_f[0:1, 7, :]), ALU.mult))
            dve.tensor_reduce(map_f[:, 2, :], map_b[:, :, :], AX_X, ALU.add)
            steps.then(dve.tensor_scalar(map_f[:, 3, :], tile_no[:, :], float(P), -float(PAD_AT), ALU.mult, ALU.add))
            steps.then(dve.tensor_tensor(map_f[:, 1, :], map_f[:, 3, :], map_f[:, 0, :], ALU.mult))
            steps.then(dve.tensor_tensor(map_f[:, 0, :], map_f[:, 1, :], map_f[:, 2, :], ALU.add))
            steps.then(dve.tensor_scalar(map_f[:, 2, :], map_f[:, 0, :], float(PAD_AT), None, ALU.add))
            dve.tensor_copy(tile_row[:, :], map_f[:, 2, :]).then_inc(map_ready, 1)
            dve.wait_ge(map_ready, 1)
            dve.wait_ge(w_moe_loaded, 48)

            def tile(j, s, turn):
                static = isinstance(j, int)
                if not (static and j >= NT):
                    m = s % 2
                    e = dve.value_load(tile_expert[0:1, ds(j, 1)], min_val=0, max_val=E - 1)
                    need(dve, hid_ready, j - 1)
                    dve.tensor_copy(w1_e[:, m, :], w1x_s[:, ds(e, 1), :].rearrange("p o f -> p (o f)")).then_inc(w1_ready, 1)
                    dve.wait_ge(x_turned, j + 1)
                    dve.tensor_copy(x_t[:, m, :], turned[m]).then_inc(x_t_ready, 1)
                if not (static and not 0 <= j - 2 < NT):
                    m, r = s % 2, (s - 2) % SLOTS
                    e = dve.value_load(tile_expert[0:1, ds(j - 2, 1)], min_val=0, max_val=E - 1)
                    dve.wait_ge(y_done, j - 1)
                    steps.then(dve.tensor_tensor(y_s[:, 0, :], expert_out[m], b2_s[:, ds(e, 1), :].rearrange("p o d -> p (o d)"), ALU.add))
                    steps.then(dve.tensor_tensor(y_s[:, 1, :], y_s[:, 0, :], rows_in[r][:, GW:GW + D], ALU.mult))
                    dve.tensor_tensor(out_s[r][:, :], y_s[:, 1, :], rows_in[r][:, X2:X2 + D], ALU.add).then_inc(out_ready, 1)

            over_tiles(dve, tile, 2, steps, 2 * SLOTS)


def _laid_out(inp):
    import numpy as np

    w_in = inp["L0_attn_w_in"].reshape(H, 3, DH, D)
    b_in = inp["L0_attn_b_in"].reshape(H, 3, DH)
    w1 = inp["L0_ffn_w1"].transpose(1, 0, 2)
    b1 = inp["L0_ffn_b1"].reshape(E, FH, P).transpose(2, 0, 1)
    experts = np.arange(E)
    arrays = {
        "x": inp["L0_attn_x"],
        "w_qkv": w_in.transpose(3, 1, 0, 2).reshape(D, 3, D),
        "b_qk": b_in[:, 0:2].transpose(0, 2, 1).reshape(D, 2),
        "b_v": b_in[:, 2].reshape(1, D),
        "w_out": inp["L0_attn_w_out"].T,
        "b_out": inp["L0_attn_b_out"].reshape(1, D),
        "router_w": inp["L0_ffn_router_w"],
        "w1x": np.concatenate([w1, b1], axis=2),
        "w2": inp["L0_ffn_w2"].reshape(E, FH, P, D).transpose(2, 0, 1, 3),
        "b2": inp["L0_ffn_b2"].reshape(1, E * D),
        "c_t": inp["L0_c"].T,
        "wmod": inp["L0_wmod"],
        "ident": np.eye(P, dtype=np.float32),
        "before": np.triu(np.ones((P, P)), 1).astype(np.float32),
        "expert_row": np.concatenate([E - experts, experts, experts * ROOM]).astype(np.float32).reshape(1, 3 * E),
        "first_row": (experts * ROOM).astype(np.float32).reshape(1, E),
        "tile_numbers": np.arange(NT, dtype=np.float32).reshape(1, NT),
        "token_numbers": np.arange(-L, 0, dtype=np.int32).reshape(LT, P).T,
    }
    return {k: np.ascontiguousarray(v) for k, v in arrays.items()}


def kernel(**inputs):
    import concourse.bacc as _bacc
    import numpy as _np
    from concourse.bass_utils import run_bass_kernel_spmd as _run

    arrays = _laid_out({k: _np.asarray(v) for k, v in inputs.items()})
    nc = _bacc.Bacc("TRN2", target_bir_lowering=False, num_devices=1)
    feeds, args = {}, []
    for name, a in arrays.items():
        feeds[f"in_{name}_dram"] = a
        args.append(nc.dram_tensor(f"in_{name}_dram", a.shape, mybir.dt.from_np(a.dtype), kind="ExternalInput").ap())
    args.append(nc.dram_tensor("out_0_dram", (B, L, D), F32, kind="ExternalOutput").ap())
    build_adaln_attention_moe(nc, *args)
    r = _run(nc, [feeds], core_ids=[0])
    return r.results[0]["out_0_dram"]
```

```python
from contextlib import ExitStack

import concourse.bass as bass
from concourse import mybir
from concourse.alu_op_type import AluOpType as ALU

F32 = mybir.dt.float32
BF16 = mybir.dt.bfloat16
I32 = mybir.dt.int32
ACT = mybir.ActivationFunctionType
AX_X = mybir.AxisListType.X
ds = bass.ds

P = 128
D = 128
B = 32
L = 256
LT = L // P
T = B * LT
NTOK = B * L
H = 16
DH = D // H
E = 14
F = 256
FH = F // P
SCALE = float(DH) ** -0.5
EPS = 1e-5

HU = 4
UNIT = [4, 4, 4, 3, 3, 3, 3, 4, 4]
UNITS = len(UNIT)
START = [sum(UNIT[:u]) for u in range(UNITS)]
RING = 3
assert sum(UNIT) == LT * H and UNITS % RING == 0 and max(UNIT) == HU

Q_PART = [0, 1, 2, 0, 1, 0]
K_PART = [0, 0, 0, 1, 1, 2]
COMBOS = len(Q_PART)

ROOM = NTOK + P
PAD_AT = E * ROOM
H2, X2, GW, ID = 0, D, 2 * D, 3 * D
ROW = 3 * D + 1
NO_TOKEN = float(1 << 20)

SLOTS = 8
NT = -(-(T + E - 1) // SLOTS) * SLOTS
W1X = F + FH

X_CHUNKS = [(0, 1), (1, 2), (2, 4), (4, B)]

MODROWS = 5


def need(eng, sem, value):
    if isinstance(value, int) and value <= 0:
        return
    eng.wait_ge(sem, value)


class Steps:

    def __init__(self, eng, sem, held):
        self.eng, self.sem, self.held, self.base, self.n = eng, sem, held, 0, 0

    def then(self, ins, plain=False):
        self.n += 1
        ins.then_inc(self.sem, 1)
        self.eng.wait_ge(self.sem, self.base + self.n)
        if plain:
            self.plain()

    def plain(self):
        self.eng.sem_inc(self.held, 1)

    def enter(self, i, per_turn):
        self.start = self.base + self.n
        self.base, self.n, self.per_turn = self.start + i * per_turn, 0, per_turn

    def leave(self, turns):
        assert self.n == self.per_turn, self.n
        self.base, self.n = self.start + turns * self.per_turn, 0


PEELED = 4
STEPS_POOL = 10
STEPS_DVE = 10


def over_batches(eng, iteration, drain, steps=None, per_turn=0, before_loop=None):
    for b in range(PEELED):
        iteration(b, b % 2)
    turns = (B - PEELED - 4) // 2
    if before_loop:
        before_loop()
    with eng.Fori(0, turns) as i:
        if steps:
            steps.enter(i, per_turn)
        iteration(2 * i + PEELED, 0)
        iteration(2 * i + PEELED + 1, 1)
    if steps:
        steps.leave(turns)
    for b in range(PEELED + 2 * turns, B):
        iteration(b, b % 2)
    drain(B, 0)


def has_tail(b):
    return not (isinstance(b, int) and b < 1)


def has_routing(b):
    return not (isinstance(b, int) and b < 2)


def has_norm(b):
    return not (isinstance(b, int) and b + 3 >= B)


def has_prep(b):
    return not (isinstance(b, int) and b + 2 >= B)


def over_tiles(eng, step, lag, steps=None, per_turn=0):
    for s in range(SLOTS):
        step(s, s, 0)
    turns = NT // SLOTS - 1
    with eng.Fori(0, turns) as i:
        if steps:
            steps.enter(i, per_turn)
        for s in range(SLOTS):
            step(SLOTS * i + SLOTS + s, s, i + 1)
    if steps:
        steps.leave(turns)
    for s in range(lag):
        step(NT + s, s, turns + 1)


def build_adaln_attention_moe(nc, x, w_qkv, b_qk, b_v, w_out, b_out, router_w, w1x, w2, b2, c_t, wmod,
                              ident, before, expert_row, first_row, tile_numbers, token_numbers, out):
    with ExitStack() as ctx:
        def sb(name, shape, dt=F32):
            return ctx.enter_context(nc.sbuf_tensor(name, shape, dt))

        def ps(name, shape, dt=F32):
            return ctx.enter_context(nc.psum_tensor(name, shape, dt))

        def sem(name):
            return ctx.enter_context(nc.semaphore(name))

        def dram(name, shape, dt=F32):
            return nc.dram_tensor(name, shape, dt, kind="Internal").ap()

        mod_rows = dram("mod_rows", (B, MODROWS * D))
        parts_dram = dram("parts_dram", (2, 2, 3, P, L), BF16)
        table = dram("table", (PAD_AT + P, ROW))

        x_tiles = x.rearrange("b (t p) d -> p (b t) d", p=P)
        out_rows = out.rearrange("b l d -> (b l) d")

        ident_s = sb("ident_s", [P, P])
        before_s = sb("before_s", [P, P], BF16)
        before_f = sb("before_f", [P, P])
        ones_s = sb("ones_s", [P, P], BF16)
        w_qkv_s = sb("w_qkv_s", [P, 3, D])
        b_qk_s = sb("b_qk_s", [P, 2])
        b_v_s = sb("b_v_s", [P, D])
        w_out_s = sb("w_out_s", [P, D])
        b_out_s = sb("b_out_s", [B, D])
        router_s = sb("router_s", [P, E])
        w1x_s = sb("w1x_s", [P, E, W1X])
        w2_s = sb("w2_s", [P, E, FH, D])
        b2_s = sb("b2_s", [P, E, D])
        expert_s = sb("expert_s", [P, 3, E])
        c_s = sb("c_s", [P, B])
        silu_s = sb("silu_s", [P, 3, B])
        wmod_s = sb("wmod_s", [P, 6 * D])
        mod_s = sb("mod_s", [B, 6 * D])
        rows_out = sb("rows_out", [B, MODROWS, D])
        mod_tmp = sb("mod_tmp", [B, 3, 2 * D])
        shift_a = sb("shift_a", [P, B])
        scale_a = sb("scale_a", [P, B])
        minus_half = sb("minus_half", [P, LT])
        eps_s = sb("eps_s", [P, LT])
        ones_row = sb("ones_row", [1, P])
        zero_s = sb("zero_s", [P, 2])
        batch_s = sb("batch_s", [P, LT], I32)
        centred1 = sb("centred1", [P, LT, D])
        centred2 = sb("centred2", [P, LT, D])
        pad_tile = sb("pad_tile", [P, ROW])
        x_s = sb("x_s", [P, T, D])
        v_s = sb("v_s", [P, T, D])
        q_stack = [sb(f"q_stack{p}", [P, H, L], BF16) for p in range(2)]
        k_stack = [sb(f"k_stack{p}", [P, H, L], BF16) for p in range(2)]
        bn1 = sb("bn1", [P, LT, 6])
        mv1 = sb("mv1", [P, LT, 2])
        rstd1 = sb("rstd1", [P, 2, LT])
        xhat1 = sb("xhat1", [P, LT, D])
        h_t = sb("h_t", [P, L])
        qk = sb("qk", [P, 2, L])
        rest = sb("rest", [P, 2, L])
        parts = sb("parts", [P, 2, 2, 3, L], BF16)
        neg_max = sb("neg_max", [P, 2, LT * H])
        exp_sum = sb("exp_sum", [P, 2, LT * H])
        att = sb("att", [P, 2, LT * H])
        mod_b = [sb(f"mod_b{p}", [P, MODROWS, D]) for p in range(2)]
        w_gated = sb("w_gated", [P, D])
        opt = sb("opt", [P, LT, D])
        opt_t = sb("opt_t", [P, L])
        bn2 = sb("bn2", [P, LT, 6])
        mv2 = sb("mv2", [P, LT, 2])
        rstd2 = sb("rstd2", [P, 2, LT])
        xhat2 = sb("xhat2", [P, LT, D])
        h_scaled = sb("h_scaled", [P, LT, D])
        h2_t = sb("h2_t", [P, L])
        rows = [sb(f"rows{p}", [P, LT, ROW]) for p in range(2)]
        top = sb("top", [P, LT])
        below = sb("below", [P, LT, E])
        exp_l = sb("exp_l", [P, LT, E])
        first = sb("first", [P, LT, E])
        rank_top = sb("rank_top", [P, LT])
        one_hot = sb("one_hot", [P, LT, E], BF16)
        weight = sb("weight", [P, 2, LT])
        place = sb("place", [P, 2, LT, E])
        place_i = [sb(f"place_i{p}", [P, LT], I32) for p in range(2)]
        next_row = sb("next_row", [P, E])
        token_id = sb("token_id", [P, LT], I32)
        count_f = sb("count_f", [P, 8, E])
        count_i = sb("count_i", [P, 2, E], I32)
        tile_no = sb("tile_no", [NT, 2])
        x_room = x_s[:, :, :].rearrange("p t d -> p (t d)")

        def reuse(offset, *shape):
            size = shape[0] if len(shape) == 1 else shape[0] * shape[1]
            part = x_room[:, offset:offset + size]
            return part if len(shape) == 1 else part.rearrange("p (a b) -> p a b", b=shape[1])

        in_expert = sb("in_expert", [NT, 3, E])
        sums_of = sb("sums_of", [NT, 3, E])
        map_p = sb("map_p", [NT, 3, E])
        map_f = sb("map_f", [NT, 5])
        expert_now = sb("expert_now", [1, NT + SLOTS], I32)
        expert_late = sb("expert_late", [1, NT + SLOTS], I32)
        tile_row = sb("tile_row", [1, NT], I32)
        end_row = sb("end_row", [1, 16], I32)
        rows_at = 0
        rows_in = [reuse(rows_at + s * ROW, ROW) for s in range(SLOTS)]
        x_t = sb("x_t", [P, 2, P])
        w1_e = sb("w1_e", [P, 2, W1X])
        hid = sb("hid", [P, 2, FH, P])
        y_s = sb("y_s", [P, 2, D])
        out_s = [reuse(rows_at + SLOTS * ROW + s * D, D) for s in range(SLOTS)]

        scores = ps("scores", [P, RING, HU * L])
        side_a = ps("side_a", [P, 512])
        side_b = ps("side_b", [P, 512])
        xhat_v = side_a[:, 0:L]
        opt_pr = side_a[:, L:2 * L]
        h2_turn = side_b[:, 0:L]
        logit_p = side_b[:, L:L + LT * E]
        rank_p = side_b[:, L + 32:L + 32 + LT * E]
        total_p = side_b[:, L + 64:L + 64 + E]
        hidden = [scores[:, 0, m * 512:m * 512 + F] for m in range(2)]
        expert_out = [scores[:, 1, m * 512:m * 512 + D] for m in range(2)]
        map_out = [side_a[0:1, n * NT:n * NT + NT] for n in range(2)]
        turned = [scores[:, 2, m * 512:m * 512 + P] for m in range(2)]

        w_in_loaded = sem("w_in_loaded")
        w_moe_loaded = sem("w_moe_loaded")
        x_loaded = [sem(f"x_loaded{n}") for n in range(len(X_CHUNKS))]
        consts_set = sem("consts_set")
        exp_c = sem("exp_c")
        silu_done = sem("silu_done")
        mod_done = sem("mod_done")
        mod_ready = sem("mod_ready")
        mod_stored = sem("mod_stored")
        mod_b_loaded = [sem("mod_b_loaded0"), sem("mod_b_loaded1")]
        pad_set = sem("pad_set")
        pad_stored = sem("pad_stored")
        dve_steps = sem("dve_steps")
        pool_steps = sem("pool_steps")
        dve_held = sem("dve_held")
        sp_held = sem("sp_held")
        pool_held = sem("pool_held")
        stats1 = sem("stats1")
        xhat1_ready = sem("xhat1_ready")
        xhat1_turned = sem("xhat1_turned")
        h_ready = sem("h_ready")
        qk_done = sem("qk_done")
        v_done = sem("v_done")
        qk_ready = sem("qk_ready")
        v_ready = sem("v_ready")
        parts_ready = sem("parts_ready")
        parts_stored = sem("parts_stored")
        stacked = [sem("stacked0"), sem("stacked1")]
        scored = sem("scored")
        maxed = sem("maxed")
        exped = sem("exped")
        att_ready = sem("att_ready")
        gated = sem("gated")
        opt_ready = sem("opt_ready")
        opt_turned = sem("opt_turned")
        opt_t_ready = sem("opt_t_ready")
        projected = sem("projected")
        stats2 = sem("stats2")
        h2_ready = sem("h2_ready")
        h2_turned = sem("h2_turned")
        h2_t_ready = sem("h2_t_ready")
        logits_done = sem("logits_done")
        below_ready = sem("below_ready")
        expl_ready = sem("expl_ready")
        hot_ready = sem("hot_ready")
        ranked = sem("ranked")
        counted = sem("counted")
        placed = sem("placed")
        weighted = sem("weighted")
        scattered = [sem("scattered0"), sem("scattered1")]
        ends_ready = sem("ends_ready")
        map_set = sem("map_set")
        map_turned = sem("map_turned")
        map_ready = sem("map_ready")
        tails_padded = sem("tails_padded")
        rows_loaded = [sem(f"rows_loaded{s}") for s in range(SLOTS)]
        x_turned = sem("x_turned")
        x_t_ready = sem("x_t_ready")
        w1_ready = sem("w1_ready")
        hid_done = sem("hid_done")
        hid_ready = sem("hid_ready")
        y_done = sem("y_done")
        out_ready = sem("out_ready")
        out_stored = [sem(f"out_stored{s}") for s in range(SLOTS)]

        LOADS_IN = 14
        SETS = 10

        block = ctx.enter_context(nc.Block())

        def load_many(eng, row, at, n, low, high):
            return nc.values_load_multi_w_load_instructions(
                row[0:1, ds(at, n)], (eng.engine,), min_val=low, max_val=high,
                skip_runtime_bounds_check_because="counts and experts are bounded by the shapes")[1]

        @block.sync
        def _(sp):
            steps = Steps(sp, sp_held, sp_held)
            sp.dma_start(c_s[:, :], c_t).then_inc(w_in_loaded, 16)
            sp.dma_start(wmod_s[:, :], wmod).then_inc(w_in_loaded, 16)

            def load_x(n):
                t = slice(LT * X_CHUNKS[n][0], LT * X_CHUNKS[n][1])
                sp.dma_start(x_s[:, t, :], x_tiles[:, t, :]).then_inc(x_loaded[n], 16)

            load_x(0)
            load_x(1)
            sp.dma_start(ident_s[:, :], ident).then_inc(w_in_loaded, 16)
            sp.dma_start(w_qkv_s[:, :, :], w_qkv).then_inc(w_in_loaded, 16)
            sp.dma_start(b_qk_s[:, :], b_qk).then_inc(w_in_loaded, 16)
            sp.dma_start(b_v_s[:, :], b_v.broadcast_to([P, D])).then_inc(w_in_loaded, 16)
            sp.dma_start(w_out_s[:, :], w_out).then_inc(w_in_loaded, 16)
            sp.dma_start(b_out_s[:, :], b_out.broadcast_to([B, D])).then_inc(w_in_loaded, 16)
            sp.dma_start(router_s[:, :], router_w).then_inc(w_in_loaded, 16)
            sp.dma_start(before_f[:, :], before).then_inc(w_in_loaded, 16)
            sp.dma_start(expert_s[:, :, :], expert_row.broadcast_to([P, 3 * E])).then_inc(w_in_loaded, 16)
            sp.dma_start(tile_no[:, :], tile_numbers).then_inc(w_in_loaded, 16)
            sp.dma_start(token_id[:, :], token_numbers).then_inc(w_in_loaded, 16)
            sp.dma_start(next_row[:, :], first_row.broadcast_to([P, E])).then_inc(w_in_loaded, 16)
            load_x(2)
            load_x(3)
            sp.wait_ge(pad_set, 2)
            sp.dma_start(table[PAD_AT:PAD_AT + P, :], pad_tile[:, :]).then_inc(pad_stored, 16)
            sp.wait_ge(mod_ready, 1)
            sp.dma_start(mod_rows, rows_out[:, :, :].rearrange("b r d -> b (r d)")).then_inc(mod_stored, 16)

            def store_parts(b, p):
                sp.wait_ge(parts_ready, b + 1)
                sp.dma_start(parts_dram[p].rearrange("q s r t -> r (q s) t"),
                             parts[:, p].rearrange("r q s t -> r (q s) t")).then_inc(parts_stored, 16)
                sp.wait_ge(parts_stored, 16 * b + 16)
                steps.plain()

            def load_stacks(b, p):
                for n, (qp, kp) in enumerate(zip(Q_PART, K_PART)):
                    r = slice(DH * n, DH * n + DH)
                    sp.dma_start(q_stack[p][r, :, :], parts_dram[p, 0, qp].rearrange("(h d) t -> d h t", d=DH)).then_inc(stacked[p], 16)
                    sp.dma_start(k_stack[p][r, :, :], parts_dram[p, 1, kp].rearrange("(h d) t -> d h t", d=DH)).then_inc(stacked[p], 16)

            sp.wait_ge(consts_set, SETS)
            for b in range(2):
                store_parts(b, b)
                load_stacks(b, b)
            sp.wait_ge(mod_stored, 16)
            sp.dma_start(w1x_s[:, :, :], w1x).then_inc(w_moe_loaded, 16)
            sp.dma_start(w2_s[:, :, :, :], w2).then_inc(w_moe_loaded, 16)
            sp.dma_start(b2_s[:, :, :], b2.broadcast_to([P, E * D])).then_inc(w_moe_loaded, 16)

            def iteration(b, p):
                need(sp, weighted, b - 1)
                sp.dma_start(mod_b[p][:, :, :], mod_rows[ds(b, 1), :].broadcast_to([P, MODROWS * D])).then_inc(mod_b_loaded[p], 16)
                if has_prep(b):
                    store_parts(b + 2, p)
                if has_prep(b):
                    sp.wait_ge(scored, UNITS * b + UNITS)
                    load_stacks(b + 2, p)

            over_batches(sp, iteration, lambda b, p: None)

            sp.wait_ge(ends_ready, 1)
            sp.wait_ge(pad_stored, 16)
            ends = load_many(sp, end_row, 0, E, 0, E * ROOM)
            for e in range(E):
                sp.dma_start(table[ds(ends[e], P), :], pad_tile[:, :]).then_inc(tails_padded, 16)
            sp.wait_ge(scattered[0], 16 * T // 2)
            sp.wait_ge(scattered[1], 16 * T // 2)
            sp.wait_ge(tails_padded, 16 * E)
            sp.wait_ge(map_ready, 1)

            def load(j, s, turn):
                if s == 0:
                    rows_of_turn[:] = load_many(sp, tile_row, SLOTS * turn, SLOTS, 0, PAD_AT)
                need(sp, out_stored[s], 16 * turn)
                sp.dma_start(rows_in[s][:, :], table[ds(rows_of_turn[s], P), :]).then_inc(rows_loaded[s], 16)

            rows_of_turn = []
            over_tiles(sp, load, 0)
            for s in range(SLOTS):
                sp.wait_ge(out_stored[s], 16 * NT // SLOTS)

        @block.gpsimd
        def _(pool):
            steps = Steps(pool, pool_steps, pool_held)
            pool.memset(ones_s[:, :], 1.0).then_inc(consts_set, 1)
            for p in range(2):
                pool.memset(q_stack[p][:, :, :], 0.0).then_inc(consts_set, 1)
                pool.memset(k_stack[p][:, :, :], 0.0).then_inc(consts_set, 1)
            pool.memset(minus_half[:, :], -0.5).then_inc(consts_set, 1)
            pool.memset(eps_s[:, :], EPS).then_inc(consts_set, 1)
            pool.memset(zero_s[:, :], 0.0).then_inc(consts_set, 1)
            pool.memset(ones_row[:, :], 1.0).then_inc(consts_set, 1)
            pool.memset(batch_s[:, :], L).then_inc(consts_set, 1)
            pool.memset(pad_tile[:, 0:ID], 0.0).then_inc(pad_set, 1)
            pool.memset(pad_tile[:, ID:ROW].bitcast(I32), int(NO_TOKEN)).then_inc(pad_set, 1)
            pool.wait_ge(consts_set, SETS)

            def normalise(mv, rstd, centred, src, dst):
                def by_token(v):
                    return v.rearrange("p (t o) -> p t o", o=1).broadcast_to([P, LT, D])

                pool.tensor_tensor(centred[:, :, :], src, mv[:, :, 0:1].broadcast_to([P, LT, D]), ALU.subtract)
                steps.then(pool.tensor_tensor(rstd[:, 0, :], mv[:, :, 1], eps_s[:, :], ALU.add))
                steps.then(pool.tensor_tensor(rstd[:, 1, :], rstd[:, 0, :], minus_half[:, :], ALU.pow))
                return pool.tensor_tensor(dst[:, :, :], centred[:, :, :], by_token(rstd[:, 1, :]), ALU.mult)

            def norm_x(b):
                pool.wait_ge(stats1, b + 1)
                need(pool, xhat1_ready, b)
                need(pool, xhat1_turned, b)
                normalise(mv1, rstd1, centred1, x_s[:, ds(LT * b, LT), :], xhat1).then_inc(xhat1_ready, 1)

            def split(b, p):
                pool.wait_ge(qk_ready, b + 1)
                need(pool, parts_stored, 16 * b - 16)
                zeros = zero_s[:, :].rearrange("p (s o) -> p s o", o=1).broadcast_to([P, 2, L])
                steps.then(pool.tensor_tensor(parts[:, p, :, 0, :], qk[:, :, :], zeros, ALU.add))
                steps.then(pool.tensor_tensor(rest[:, :, :], qk[:, :, :], parts[:, p, :, 0, :], ALU.subtract))
                steps.then(pool.tensor_tensor(parts[:, p, :, 1, :], rest[:, :, :], zeros, ALU.add))
                pool.tensor_tensor(parts[:, p, :, 2, :], rest[:, :, :], parts[:, p, :, 1, :], ALU.subtract).then_inc(parts_ready, 1)

            def gate(b, p):
                pool.wait_ge(mod_b_loaded[p], 8 * (b - p) + 16)
                need(pool, projected, b)
                pool.tensor_tensor(w_gated[:, :], w_out_s[:, :], mod_b[p][:, 0, :], ALU.mult).then_inc(gated, 1)

            def attend(b, p):
                pool.wait_ge(att_ready, b + 1)
                need(pool, opt_turned, b)
                for t in range(LT):
                    last = pool.tensor_tensor(
                        opt[:, t, :].rearrange("p (h d) -> p h d", d=DH),
                        v_s[:, ds(LT * b + t, 1), :].rearrange("p t (h d) -> p (t h) d", d=DH),
                        att[:, 1, t * H:t * H + H].rearrange("p (h o) -> p h o", o=1).broadcast_to([P, H, DH]),
                        ALU.mult)
                last.then_inc(opt_ready, 1)

            def norm_x2(b, p):
                pool.wait_ge(stats2, b + 1)
                need(pool, scattered[p], 8 * LT * (b - p))
                steps.then(normalise(mv2, rstd2, centred2, rows[p][:, :, X2:X2 + D], xhat2))
                steps.then(pool.tensor_tensor(h_scaled[:, :, :], xhat2[:, :, :],
                                              mod_b[p][:, 2:3, :].broadcast_to([P, LT, D]), ALU.mult))
                pool.tensor_tensor(rows[p][:, :, H2:H2 + D], h_scaled[:, :, :],
                                   mod_b[p][:, 3:4, :].broadcast_to([P, LT, D]), ALU.add).then_inc(h2_ready, 1)

            def scatter(b, p):
                pool.wait_ge(placed, b + 1)
                pool.tensor_tensor(rows[p][:, :, ID:ROW].bitcast(I32), token_id[:, :].rearrange("p (t o) -> p t o", o=1),
                                   batch_s[:, :].rearrange("p (t o) -> p t o", o=1), ALU.add)
                steps.then(pool.tensor_tensor(token_id[:, :], token_id[:, :], batch_s[:, :], ALU.add))
                pool.tensor_tensor(rows[p][:, :, GW:GW + D], mod_b[p][:, 4:5, :].broadcast_to([P, LT, D]),
                                   weight[:, 1, :].rearrange("p (t o) -> p t o", o=1).broadcast_to([P, LT, D]),
                                   ALU.mult).then_inc(weighted, 1)
                pool.wait_ge(weighted, b + 1)
                steps.plain()
                for t in range(LT):
                    pool.indirect_dma_start(table, bass.IndirectOffsetOnAxis(ap=place_i[p][:, t:t + 1], axis=0),
                                            rows[p][:, t, :], None).then_inc(scattered[p], 16)

            pool.wait_ge(w_in_loaded, 16 * LOADS_IN)
            for b in range(2):
                norm_x(b)
                split(b, b)
            norm_x(2)

            def iteration(b, p):
                if has_tail(b):
                    gate(b - 1, 1 - p)
                    attend(b - 1, 1 - p)
                if has_norm(b):
                    norm_x(b + 3)
                if has_routing(b):
                    scatter(b - 2, p)
                if has_tail(b):
                    norm_x2(b - 1, 1 - p)
                if has_prep(b):
                    split(b + 2, p)

            def drain(b, p):
                gate(b - 1, 1 - p)
                attend(b - 1, 1 - p)
                scatter(b - 2, p)
                norm_x2(b - 1, 1 - p)
                scatter(b - 1, 1 - p)

            over_batches(pool, iteration, drain, steps, 2 * STEPS_POOL)

            def store(j, s, turn):
                pool.wait_ge(out_ready, j + 1)
                steps.plain()
                pool.indirect_dma_start(out_rows, bass.IndirectOffsetOnAxis(ap=rows_in[s][:, ID:ROW].bitcast(I32), axis=0),
                                        out_s[s][:, :], None, bounds_check=NTOK - 1, oob_is_err=False).then_inc(out_stored[s], 16)

            over_tiles(pool, store, 0)

        @block.scalar
        def _(act):
            act.wait_ge(w_in_loaded, 16 * LOADS_IN)
            act.activation(silu_s[:, 0, :], c_s[:, :], ACT.Exp, scale=-1.0).then_inc(exp_c, 1)

            def iteration(b, p):
                for u in range(UNITS):
                    act.wait_ge(maxed, UNITS * b + u + 1)
                    buf = scores[:, u % RING, :]
                    for k in range(UNIT[u]):
                        n = START[u] + k
                        last = act.activation(buf[:, k * L:k * L + L], buf[:, k * L:k * L + L], ACT.Exp,
                                              bias=neg_max[:, p, n:n + 1], accum_out=exp_sum[:, p, n:n + 1])
                    last.then_inc(exped, 1)
                    if u == 3 and has_routing(b):
                        router_exp(b - 2)

            def router_exp(b):
                act.wait_ge(below_ready, b + 1)
                act.activation(exp_l[:, :, :], below[:, :, :], ACT.Exp).then_inc(expl_ready, 1)

            def drain(b, p):
                router_exp(b - 2)
                router_exp(b - 1)

            over_batches(act, iteration, drain)

            def gelu(j, s, turn):
                if not (isinstance(j, int) and j >= NT):
                    act.wait_ge(x_turned, j + 1)
                    need(act, hid_done, j - 1)
                    act.copy(x_t[:, s % 2, :], turned[s % 2]).then_inc(x_t_ready, 1)
                if isinstance(j, int) and j < 1:
                    return
                m = (s - 1) % 2
                act.wait_ge(hid_done, j)
                need(act, y_done, j - 2)
                for f in range(FH):
                    last = act.activation(hid[:, m, f, :], hidden[m][:, f * P:f * P + P], ACT.Gelu,
                                          bias=w1_e[:, m, F + f:F + f + 1])
                last.then_inc(hid_ready, 1)

            over_tiles(act, gelu, 1)

        @block.tensor
        def _(pe):
            pe.wait_ge(silu_done, 1)
            pe.wait_ge(w_in_loaded, 16 * LOADS_IN)
            silu = silu_s[:, 2, :]
            for n in range(2):
                pe.matmul(scores[0:B, 0, n * 512:n * 512 + 3 * D], silu, wmod_s[:, n * 3 * D:(n + 1) * 3 * D], start=True, stop=True)
            for n in range(2):
                last = pe.matmul(scores[:, 1, n * 512:n * 512 + B], wmod_s[:, n * D:n * D + D], silu, start=True, stop=True)
            last.then_inc(mod_done, 1)

            def turn_x(b):
                pe.wait_ge(xhat1_ready, b + 1)
                need(pe, v_ready, b)
                need(pe, stats2, b - 3)
                for t in range(LT):
                    last = pe.transpose(xhat_v[:, t * P:t * P + P], xhat1[:, t, :], ident_s[:, :])
                last.then_inc(xhat1_turned, 1)

            def project_v(b):
                pe.wait_ge(h_ready, b + 1)
                for t in range(LT):
                    last = pe.matmul(xhat_v[:, t * P:t * P + P], h_t[:, t * P:t * P + P], w_qkv_s[:, 2, :], start=True, stop=True)
                last.then_inc(v_done, 1)

            def project_qk(b):
                need(pe, counted, b - 3)
                need(pe, qk_ready, b)
                for n in range(2):
                    last = pe.matmul(side_b[:, n * L:n * L + L], w_qkv_s[:, n, :], h_t[:, :], start=True, stop=True)
                last.then_inc(qk_done, 1)

            def score(b, p, u):
                if u == 0:
                    pe.wait_ge(stacked[p], (2 * 16 * COMBOS // 2) * (b - p) + 2 * 16 * COMBOS)
                need(pe, exped, UNITS * b + u - RING + 1)
                for k in range(UNIT[u]):
                    t, h = (START[u] + k) // H, (START[u] + k) % H
                    last = pe.matmul(scores[:, u % RING, k * L:k * L + L], q_stack[p][:, h, t * P:t * P + P],
                                     k_stack[p][:, h, :], start=True, stop=True)
                last.then_inc(scored, 1)

            def turn_opt(b, ahead):
                pe.wait_ge(opt_ready, b + 1)
                need(pe, stats2, b)
                pe.wait_ge(v_ready, ahead)
                for t in range(LT):
                    last = pe.transpose(opt_pr[:, t * P:t * P + P], opt[:, t, :], ident_s[:, :])
                last.then_inc(opt_turned, 1)

            def project_out(b, p):
                pe.wait_ge(opt_t_ready, b + 1)
                pe.wait_ge(gated, b + 1)
                for t in range(LT):
                    pe.matmul(opt_pr[:, t * P:t * P + P], opt_t[:, t * P:t * P + P], w_gated[:, :], start=True, stop=False)
                    last = pe.matmul(opt_pr[:, t * P:t * P + P], ones_row[:, :], mod_b[p][0:1, 1, :], start=False, stop=True)
                last.then_inc(projected, 1)

            def turn_h2(b, p, ahead):
                pe.wait_ge(h2_ready, b + 1)
                need(pe, counted, b)
                pe.wait_ge(qk_ready, ahead)
                for t in range(LT):
                    last = pe.transpose(h2_turn[:, t * P:t * P + P], rows[p][:, t, H2:H2 + D], ident_s[:, :])
                last.then_inc(h2_turned, 1)

            def route(b):
                pe.wait_ge(h2_t_ready, b + 1)
                for t in range(LT):
                    last = pe.matmul(logit_p[:, t * E:t * E + E], h2_t[:, t * P:t * P + P], router_s[:, :], start=True, stop=True)
                last.then_inc(logits_done, 1)

            def rank(b):
                pe.wait_ge(hot_ready, b + 1)
                pe.matmul(rank_p[:, 0:E], before_s[:, :], one_hot[:, 0, :], start=True, stop=True)
                pe.matmul(rank_p[:, E:2 * E], before_s[:, :], one_hot[:, 1, :], start=True, stop=False)
                pe.matmul(rank_p[:, E:2 * E], ones_s[:, :], one_hot[:, 0, :], start=False, stop=True)
                pe.matmul(total_p, ones_s[:, :], one_hot[:, 0, :], start=True, stop=False)
                pe.matmul(total_p, ones_s[:, :], one_hot[:, 1, :], start=False, stop=True).then_inc(ranked, 1)

            pe.wait_ge(w_in_loaded, 16 * LOADS_IN)
            pe.wait_ge(mod_ready, 1)
            for b in range(2):
                turn_x(b)
                project_v(b)
                project_qk(b)

            def up_to(b):
                return min(b, B) if isinstance(b, int) else b

            def iteration(b, p):
                score(b, p, 0)
                if has_prep(b):
                    turn_x(b + 2)
                score(b, p, 1)
                if has_prep(b):
                    project_v(b + 2)
                if has_routing(b):
                    turn_h2(b - 2, p, up_to(b + 2))
                score(b, p, 2)
                if has_routing(b):
                    route(b - 2)
                score(b, p, 3)
                score(b, p, 4)
                if has_tail(b):
                    turn_opt(b - 1, up_to(b + 3))
                if has_routing(b):
                    rank(b - 2)
                score(b, p, 5)
                if has_tail(b):
                    project_out(b - 1, 1 - p)
                score(b, p, 6)
                if has_prep(b):
                    project_qk(b + 2)
                score(b, p, 7)
                score(b, p, 8)

            def drain(b, p):
                turn_h2(b - 2, p, B)
                route(b - 2)
                rank(b - 2)
                turn_opt(b - 1, B)
                project_out(b - 1, 1 - p)
                turn_h2(b - 1, 1 - p, B)
                route(b - 1)
                rank(b - 1)

            over_batches(pe, iteration, drain)

            pe.wait_ge(map_set, 1)
            for n in range(2):
                last = pe.matmul(map_out[n], map_f[:, 3 + n:4 + n], ident_s[0:NT, 0:NT], start=True, stop=True)
            last.then_inc(map_turned, 1)
            pe.wait_ge(map_ready, 1)
            pe.wait_ge(w_moe_loaded, 48)
            experts = []

            def tile(j, s, turn):
                static = isinstance(j, int)
                if s == 0:
                    experts[:] = load_many(pe, expert_late, SLOTS * turn, SLOTS, 0, E - 1)
                if not (static and j >= NT):
                    pe.wait_ge(rows_loaded[s], 16 * turn + 16)
                    need(pe, x_t_ready, j - 1)
                    pe.transpose(turned[s % 2], rows_in[s][:, H2:H2 + D], ident_s[:, :]).then_inc(x_turned, 1)
                if not (static and not 0 <= j - 1 < NT):
                    m = (s - 1) % 2
                    pe.wait_ge(x_t_ready, j)
                    pe.wait_ge(w1_ready, j)
                    need(pe, hid_ready, j - 2)
                    for f in range(FH):
                        last = pe.matmul(hidden[m][:, f * P:f * P + P], w1_e[:, m, f * P:f * P + P], x_t[:, m, :], start=True, stop=True)
                    last.then_inc(hid_done, 1)
                if not (static and not 0 <= j - 2 < NT):
                    m = s % 2
                    pe.wait_ge(hid_ready, j - 1)
                    need(pe, out_ready, j - 3)
                    for f in range(FH):
                        last = pe.matmul(expert_out[m], hid[:, m, f, :], w2_s[:, ds(experts[s], 1), f, :], start=(f == 0), stop=(f == FH - 1))
                    last.then_inc(y_done, 1)

            over_tiles(pe, tile, 2)

        @block.vector
        def _(dve):
            steps = Steps(dve, dve_steps, dve_held)
            dve.wait_ge(exp_c, 1)
            steps.then(dve.tensor_scalar(silu_s[:, 0, :], silu_s[:, 0, :], 1.0, None, ALU.add))
            steps.then(dve.reciprocal(silu_s[:, 1, :], silu_s[:, 0, :]))
            dve.tensor_tensor(silu_s[:, 2, :], c_s[:, :], silu_s[:, 1, :], ALU.mult).then_inc(silu_done, 1)
            dve.wait_ge(w_in_loaded, 16 * LOADS_IN)
            dve.tensor_copy(before_s[:, :], before_f[:, :])
            dve.tensor_scalar(w_qkv_s[:, 0, :], w_qkv_s[:, 0, :], SCALE, None, ALU.mult)
            dve.tensor_scalar(b_qk_s[:, 0:1], b_qk_s[:, 0:1], SCALE, None, ALU.mult)
            dve.wait_ge(mod_done, 1)
            for n in range(2):
                dve.tensor_copy(mod_s[:, n * 3 * D:(n + 1) * 3 * D], scores[0:B, 0, n * 512:n * 512 + 3 * D])
            dve.tensor_copy(shift_a[:, :], scores[:, 1, 0:B])
            steps.then(dve.tensor_scalar(scale_a[:, :], scores[:, 1, 512:512 + B], 1.0, None, ALU.add))
            for n, chunk in enumerate((2, 5)):
                g = mod_s[:, chunk * D:chunk * D + D]
                w = slice(n * D, n * D + D)
                steps.then(dve.tensor_scalar(mod_tmp[:, 0, w], g, 0.0, 2.0, ALU.is_ge, ALU.mult))
                steps.then(dve.tensor_scalar(mod_tmp[:, 1, w], g, -1.0, None, ALU.mult))
                steps.then(dve.tensor_tensor(mod_tmp[:, 2, w], mod_tmp[:, 1, w], g, ALU.max))
                steps.then(dve.tensor_scalar(mod_tmp[:, 1, w], mod_tmp[:, 2, w], 0.25, None, ALU.max))
                steps.then(dve.tensor_scalar(mod_tmp[:, 2, w], mod_tmp[:, 0, w], -1.0, None, ALU.add))
                steps.then(dve.tensor_tensor(rows_out[:, (0, 4)[n], :], mod_tmp[:, 1, w], mod_tmp[:, 2, w], ALU.mult))
            dve.tensor_tensor(rows_out[:, 1, :], rows_out[:, 0, :], b_out_s[:, :], ALU.mult)
            dve.tensor_scalar(rows_out[:, 2, :], mod_s[:, 4 * D:5 * D], 1.0, None, ALU.add)
            dve.tensor_copy(rows_out[:, 3, :], mod_s[:, 3 * D:4 * D]).then_inc(mod_ready, 1)

            def stats(src, bn, mv):
                for t in range(LT):
                    ins = dve.bn_stats(bn[:, t, :], src(t))
                steps.then(ins, plain=True)
                for t in range(LT):
                    last = dve.bn_aggr(mv[:, t, :], bn[:, t, :])
                return last

            def stats_x(b, p):
                if isinstance(b, int):
                    dve.wait_ge(x_loaded[next(n for n, c in enumerate(X_CHUNKS) if c[0] <= b < c[1])], 16)
                need(dve, xhat1_ready, b)
                stats(lambda t: x_s[:, ds(LT * b + t, 1), :].rearrange("p t d -> p (t d)"), bn1, mv1).then_inc(stats1, 1)

            def make_h(b):
                dve.wait_ge(xhat1_turned, b + 1)
                dve.tensor_scalar(h_t[:, :], xhat_v, scale_a[:, ds(b, 1)], shift_a[:, ds(b, 1)], ALU.mult, ALU.add).then_inc(h_ready, 1)

            def take_qk(b):
                dve.wait_ge(qk_done, b + 1)
                need(dve, parts_ready, b)
                dve.tensor_tensor(qk[:, :, :], side_b[:, :].rearrange("p (s t) -> p s t", s=2),
                                  b_qk_s[:, :].rearrange("p (s o) -> p s o", o=1).broadcast_to([P, 2, L]), ALU.add).then_inc(qk_ready, 1)

            def take_v(b):
                dve.wait_ge(v_done, b + 1)
                dve.tensor_tensor(v_s[:, ds(LT * b, LT), :], xhat_v.rearrange("p (t d) -> p t d", t=LT),
                                  b_v_s[:, :].rearrange("p (o d) -> p o d", o=1).broadcast_to([P, LT, D]), ALU.add).then_inc(v_ready, 1)

            def row_max(b, p, u):
                dve.wait_ge(scored, UNITS * b + u + 1)
                dve.tensor_reduce(neg_max[:, p, START[u]:START[u] + UNIT[u]],
                                  scores[:, u % RING, 0:UNIT[u] * L].rearrange("p (h m) -> p h m", m=L),
                                  AX_X, ALU.max, negate=True).then_inc(maxed, 1)

            def attention_sums(b, p):
                dve.wait_ge(exped, UNITS * b + UNITS)
                need(dve, opt_ready, b)
                steps.then(dve.reciprocal(att[:, 0, :], exp_sum[:, p, :]))
                dve.tensor_tensor(att[:, 1, :], exp_sum[:, p, :], att[:, 0, :], ALU.mult).then_inc(att_ready, 1)

            def take_opt(b):
                dve.wait_ge(opt_turned, b + 1)
                dve.tensor_copy(opt_t[:, :], opt_pr).then_inc(opt_t_ready, 1)

            def residual(b, p):
                dve.wait_ge(projected, b + 1)
                need(dve, scattered[p], 8 * LT * (b - p))
                steps.then(dve.tensor_tensor(rows[p][:, :, X2:X2 + D], opt_pr.rearrange("p (t d) -> p t d", t=LT),
                                             x_s[:, ds(LT * b, LT), :], ALU.add))
                need(dve, h2_ready, b)
                stats(lambda t: rows[p][:, t, X2:X2 + D], bn2, mv2).then_inc(stats2, 1)

            def take_h2(b):
                dve.wait_ge(h2_turned, b + 1)
                dve.tensor_copy(h2_t[:, :], h2_turn).then_inc(h2_t_ready, 1)

            def bcast(v):
                return v.rearrange("p (t o) -> p t o", o=1).broadcast_to([P, LT, E])

            def per_tile(v):
                return v.rearrange("p (o e) -> p o e", o=1).broadcast_to([P, LT, E])

            def choose(b):
                dve.wait_ge(logits_done, b + 1)
                logits = logit_p.rearrange("p (t e) -> p t e", t=LT)
                steps.then(dve.tensor_reduce(top[:, :], logits, AX_X, ALU.max))
                dve.tensor_tensor(below[:, :, :], logits, bcast(top[:, :]), ALU.subtract).then_inc(below_ready, 1)
                dve.wait_ge(below_ready, b + 1)
                steps.then(dve.scalar_tensor_tensor(out=first[:, :, :], in0=below[:, :, :], scalar=0.0,
                                                    in1=per_tile(expert_s[:, 0, :]), op0=ALU.is_ge, op1=ALU.mult))
                steps.then(dve.tensor_reduce(rank_top[:, :], first[:, :, :], AX_X, ALU.max))
                dve.tensor_tensor(one_hot[:, :, :], first[:, :, :], bcast(rank_top[:, :]), ALU.is_equal).then_inc(hot_ready, 1)

            def find_place(b, p):
                dve.wait_ge(ranked, b + 1)
                steps.then(dve.tensor_tensor(place[:, 0], rank_p.rearrange("p (t e) -> p t e", t=LT), per_tile(next_row[:, :]), ALU.add))
                dve.tensor_tensor(next_row[:, :], next_row[:, :], total_p, ALU.add).then_inc(counted, 1)
                steps.then(dve.tensor_tensor(place[:, 1], place[:, 0], one_hot[:, :, :], ALU.mult))
                dve.tensor_reduce(place_i[p][:, :], place[:, 1], AX_X, ALU.max)
                dve.wait_ge(expl_ready, b + 1)
                steps.then(dve.tensor_reduce(weight[:, 0, :], exp_l[:, :, :], AX_X, ALU.add))
                need(dve, weighted, b)
                dve.reciprocal(weight[:, 1, :], weight[:, 0, :]).then_inc(placed, 1)

            for b in range(2):
                stats_x(b, b)
                make_h(b)
                take_v(b)
                take_qk(b)
            stats_x(2, 0)

            def iteration(b, p):
                row_max(b, p, 0)
                if has_prep(b):
                    make_h(b + 2)
                row_max(b, p, 1)
                if has_routing(b):
                    take_h2(b - 2)
                if has_prep(b):
                    take_v(b + 2)
                row_max(b, p, 2)
                if has_tail(b):
                    attention_sums(b - 1, 1 - p)
                row_max(b, p, 3)
                if has_routing(b):
                    choose(b - 2)
                row_max(b, p, 4)
                if has_tail(b):
                    take_opt(b - 1)
                if has_norm(b):
                    stats_x(b + 3, 1 - p)
                row_max(b, p, 5)
                if has_routing(b):
                    find_place(b - 2, p)
                row_max(b, p, 6)
                if has_tail(b):
                    residual(b - 1, 1 - p)
                row_max(b, p, 7)
                if has_prep(b):
                    take_qk(b + 2)
                row_max(b, p, 8)

            def drain(b, p):
                attention_sums(b - 1, 1 - p)
                take_h2(b - 2)
                choose(b - 2)
                find_place(b - 2, p)
                take_opt(b - 1)
                residual(b - 1, 1 - p)
                take_h2(b - 1)
                choose(b - 1)
                find_place(b - 1, 1 - p)

            over_batches(dve, iteration, drain, steps, 2 * STEPS_DVE, lambda: dve.wait_ge(x_loaded[3], 16))

            first_e = expert_s[:, 2, :]
            dve.wait_ge(counted, B)
            dve.tensor_copy(end_row[:, 0:E], next_row[0:1, :]).then_inc(ends_ready, 1)
            steps.then(dve.tensor_tensor(count_f[:, 0, :], next_row[:, :], first_e, ALU.subtract))
            steps.then(dve.tensor_scalar(count_i[:, 0, :], count_f[:, 0, :], float(P - 1), None, ALU.add))
            steps.then(dve.tensor_scalar(count_i[:, 1, :], count_i[:, 0, :], P.bit_length() - 1, None, ALU.arith_shift_right))
            steps.then(dve.tensor_copy(count_f[:, 2, :], count_i[:, 1, :]))
            at, shift = 2, 1
            while shift < E:
                to = {2: 3, 3: 4, 4: 3}[at]
                dve.tensor_copy(count_f[:, to, 0:shift], count_f[:, at, 0:shift])
                steps.then(dve.tensor_tensor(count_f[:, to, shift:E], count_f[:, at, shift:E], count_f[:, at, 0:E - shift], ALU.add))
                at, shift = to, 2 * shift
            steps.then(dve.tensor_tensor(count_f[:, 5, :], count_f[:, at, :], count_f[:, 2, :], ALU.subtract))
            steps.then(dve.tensor_scalar(count_f[:, 6, :], count_f[:, 5, :], -float(P), None, ALU.mult))
            dve.tensor_tensor(sums_of[:, 2, :], count_f[0:NT, 6, :], first_e[0:NT], ALU.add)
            dve.memset(sums_of[:, 0, :], 1.0)
            dve.tensor_copy(sums_of[:, 1, :], expert_s[0:NT, 1, :])
            tile = tile_no[:, 1:2].broadcast_to([NT, E])
            dve.tensor_tensor(in_expert[:, 0, :], tile, count_f[0:NT, 5, :], ALU.is_ge)
            steps.then(dve.tensor_tensor(in_expert[:, 1, :], tile, count_f[0:NT, at, :], ALU.is_ge))
            steps.then(dve.tensor_tensor(in_expert[:, 2, :], in_expert[:, 0, :], in_expert[:, 1, :], ALU.subtract))
            steps.then(dve.tensor_tensor(map_p[:, :, :], in_expert[:, 2:3, :].broadcast_to([NT, 3, E]), sums_of[:, :, :], ALU.mult))
            steps.then(dve.tensor_reduce(map_f[:, 0:3], map_p[:, :, :], AX_X, ALU.add))
            dve.tensor_copy(map_f[:, 3:4], map_f[:, 1:2])
            steps.then(dve.tensor_tensor(map_p[:, 0, 0:1], tile_no[:, 0:1], map_f[:, 0:1], ALU.mult))
            dve.tensor_tensor(map_f[:, 4:5], map_p[:, 0, 0:1], map_f[:, 2:3], ALU.add).then_inc(map_set, 1)
            for v in (expert_now, expert_late):
                steps.then(dve.memset(v[:, :], 0))
            dve.wait_ge(map_turned, 1)
            dve.tensor_copy(expert_now[:, 0:NT], map_out[0])
            dve.tensor_copy(expert_late[:, 2:NT + 2], map_out[0])
            dve.tensor_scalar(tile_row[:, :], map_out[1], float(PAD_AT), None, ALU.add).then_inc(map_ready, 1)
            dve.wait_ge(map_ready, 1)
            dve.wait_ge(w_moe_loaded, 48)
            now, late = [], []

            def tile(j, s, turn):
                static = isinstance(j, int)
                if s == 0:
                    now[:] = load_many(dve, expert_now, SLOTS * turn, SLOTS, 0, E - 1)
                    late[:] = load_many(dve, expert_late, SLOTS * turn, SLOTS, 0, E - 1)
                if not (static and j >= NT):
                    m = s % 2
                    need(dve, hid_ready, j - 1)
                    dve.tensor_copy(w1_e[:, m, :], w1x_s[:, ds(now[s], 1), :].rearrange("p o f -> p (o f)")).then_inc(w1_ready, 1)
                if not (static and not 0 <= j - 2 < NT):
                    m, r = s % 2, (s - 2) % SLOTS
                    dve.wait_ge(y_done, j - 1)
                    steps.then(dve.tensor_tensor(y_s[:, 0, :], expert_out[m], b2_s[:, ds(late[s], 1), :].rearrange("p o d -> p (o d)"), ALU.add))
                    steps.then(dve.tensor_tensor(y_s[:, 1, :], y_s[:, 0, :], rows_in[r][:, GW:GW + D], ALU.mult))
                    dve.tensor_tensor(out_s[r][:, :], y_s[:, 1, :], rows_in[r][:, X2:X2 + D], ALU.add).then_inc(out_ready, 1)

            over_tiles(dve, tile, 2, steps, 2 * SLOTS)


def _laid_out(inp):
    import numpy as np

    w_in = inp["L0_attn_w_in"].reshape(H, 3, DH, D)
    b_in = inp["L0_attn_b_in"].reshape(H, 3, DH)
    w1 = inp["L0_ffn_w1"].transpose(1, 0, 2)
    b1 = inp["L0_ffn_b1"].reshape(E, FH, P).transpose(2, 0, 1)
    experts = np.arange(E)
    arrays = {
        "x": inp["L0_attn_x"],
        "w_qkv": w_in.transpose(3, 1, 0, 2).reshape(D, 3, D),
        "b_qk": b_in[:, 0:2].transpose(0, 2, 1).reshape(D, 2),
        "b_v": b_in[:, 2].reshape(1, D),
        "w_out": inp["L0_attn_w_out"].T,
        "b_out": inp["L0_attn_b_out"].reshape(1, D),
        "router_w": inp["L0_ffn_router_w"],
        "w1x": np.concatenate([w1, b1], axis=2),
        "w2": inp["L0_ffn_w2"].reshape(E, FH, P, D).transpose(2, 0, 1, 3),
        "b2": inp["L0_ffn_b2"].reshape(1, E * D),
        "c_t": inp["L0_c"].T,
        "wmod": inp["L0_wmod"],
        "ident": np.eye(P, dtype=np.float32),
        "before": np.triu(np.ones((P, P)), 1).astype(np.float32),
        "expert_row": np.concatenate([E - experts, experts, experts * ROOM]).astype(np.float32).reshape(1, 3 * E),
        "first_row": (experts * ROOM).astype(np.float32).reshape(1, E),
        "tile_numbers": np.stack([P * np.arange(NT) - PAD_AT, np.arange(NT)], axis=1).astype(np.float32),
        "token_numbers": np.arange(-L, 0, dtype=np.int32).reshape(LT, P).T,
    }
    return {k: np.ascontiguousarray(v) for k, v in arrays.items()}


def kernel(**inputs):
    import concourse.bacc as _bacc
    import numpy as _np
    from concourse.bass_utils import run_bass_kernel_spmd as _run

    arrays = _laid_out({k: _np.asarray(v) for k, v in inputs.items()})
    nc = _bacc.Bacc("TRN2", target_bir_lowering=False, num_devices=1)
    feeds, args = {}, []
    for name, a in arrays.items():
        feeds[f"in_{name}_dram"] = a
        args.append(nc.dram_tensor(f"in_{name}_dram", a.shape, mybir.dt.from_np(a.dtype), kind="ExternalInput").ap())
    args.append(nc.dram_tensor("out_0_dram", (B, L, D), F32, kind="ExternalOutput").ap())
    build_adaln_attention_moe(nc, *args)
    r = _run(nc, [feeds], core_ids=[0])
    return r.results[0]["out_0_dram"]
```

```python
from contextlib import ExitStack

import concourse.bass as bass
from concourse import mybir
from concourse.alu_op_type import AluOpType as ALU

F32 = mybir.dt.float32
BF16 = mybir.dt.bfloat16
I32 = mybir.dt.int32
ACT = mybir.ActivationFunctionType
AX_X = mybir.AxisListType.X
ds = bass.ds

P = 128
D = 128
B = 32
L = 256
LT = L // P
T = B * LT
NTOK = B * L
H = 16
DH = D // H
E = 14
F = 256
FH = F // P
SCALE = float(DH) ** -0.5
EPS = 1e-5

HU = 4
UNIT = [3, 4, 3, 4, 3, 3, 4, 4, 4]
UNITS = len(UNIT)
START = [sum(UNIT[:u]) for u in range(UNITS)]
RING = 3
assert sum(UNIT) == LT * H and UNITS % RING == 0 and max(UNIT) == HU

Q_PART = [0, 1, 2, 0, 1, 0]
K_PART = [0, 0, 0, 1, 1, 2]
COMBOS = len(Q_PART)

ROOM = NTOK + P
PAD_AT = E * ROOM
H2, X2, GW, ID = 0, D, 2 * D, 3 * D
ROW = 3 * D + 1
NO_TOKEN = float(1 << 20)

SLOTS = 16
NT = -(-(T + E - 1) // SLOTS) * SLOTS
AT_W1, AT_W2, AT_OUT = 2, 4, 5
BUFS = 4
W1X = F + FH

X_CHUNKS = [(0, 1), (1, 2), (2, 4), (4, B)]

MODROWS = 5


def need(eng, sem, value):
    if isinstance(value, int) and value <= 0:
        return
    eng.wait_ge(sem, value)


class Steps:

    def __init__(self, eng, sem, held):
        self.eng, self.sem, self.held, self.base, self.n = eng, sem, held, 0, 0

    def then(self, ins):
        self.after(self.did(ins))

    def did(self, ins):
        self.n += 1
        ins.then_inc(self.sem, 1)
        return self.n

    def after(self, n, plain=False):
        self.eng.wait_ge(self.sem, self.base + n)
        if plain:
            self.plain()

    def plain(self):
        self.eng.sem_inc(self.held, 1)

    def enter(self, i, per_turn):
        self.start = self.base + self.n
        self.base, self.n, self.per_turn = self.start + i * per_turn, 0, per_turn

    def leave(self, turns):
        assert self.n == self.per_turn, self.n
        self.base, self.n = self.start + turns * self.per_turn, 0


PEELED = 4
TURN = 4
STEPS_POOL = 10
STEPS_DVE = 10


def over_batches(eng, iteration, drain, steps=None, per_turn=0, before_loop=None):
    for b in range(PEELED):
        iteration(b, b % 2)
    turns = (B - PEELED - 4) // TURN
    if before_loop:
        before_loop()
    with eng.Fori(0, turns) as i:
        if steps:
            steps.enter(i, per_turn)
        for n in range(TURN):
            iteration(TURN * i + PEELED + n, n % 2)
    if steps:
        steps.leave(turns)
    for b in range(PEELED + TURN * turns, B):
        iteration(b, b % 2)
    drain(B, 0)


def has_tail(b):
    return not (isinstance(b, int) and b < 1)


def has_routing(b):
    return not (isinstance(b, int) and b < 2)


def has_norm(b):
    return not (isinstance(b, int) and b + 3 >= B)


def has_prep(b):
    return not (isinstance(b, int) and b + 2 >= B)


def in_range(j):
    return not isinstance(j, int) or 0 <= j < NT


def over_tiles(eng, step, lag):
    for s in range(SLOTS):
        step(s, s, 0)
    turns = NT // SLOTS - 1
    with eng.Fori(0, turns) as i:
        for s in range(SLOTS):
            step(SLOTS * i + SLOTS + s, s, i + 1)
    for s in range(lag):
        step(NT + s, s, turns + 1)


def build_adaln_attention_moe(nc, x, w_qkv, b_qk, b_v, w_out, b_out, router_w, w1x, w2, b2, c_t, wmod,
                              ident, before, expert_row, first_row, tile_numbers, token_numbers, out):
    with ExitStack() as ctx:
        def sb(name, shape, dt=F32):
            return ctx.enter_context(nc.sbuf_tensor(name, shape, dt))

        def ps(name, shape, dt=F32):
            return ctx.enter_context(nc.psum_tensor(name, shape, dt))

        def sem(name):
            return ctx.enter_context(nc.semaphore(name))

        def dram(name, shape, dt=F32):
            return nc.dram_tensor(name, shape, dt, kind="Internal").ap()

        mod_rows = dram("mod_rows", (B, MODROWS * D))
        parts_dram = dram("parts_dram", (2, 2, 3, P, L), BF16)
        table = dram("table", (PAD_AT + P, ROW))

        x_tiles = x.rearrange("b (t p) d -> p (b t) d", p=P)
        out_rows = out.rearrange("b l d -> (b l) d")

        ident_s = sb("ident_s", [P, P])
        before_s = sb("before_s", [P, P], BF16)
        before_f = sb("before_f", [P, P])
        ones_s = sb("ones_s", [P, P], BF16)
        w_qkv_s = sb("w_qkv_s", [P, 3, D])
        b_qk_s = sb("b_qk_s", [P, 2])
        b_v_s = sb("b_v_s", [P, D])
        w_out_s = sb("w_out_s", [P, D])
        b_out_s = sb("b_out_s", [B, D])
        router_s = sb("router_s", [P, E])
        w1x_s = sb("w1x_s", [P, E, W1X])
        w2_s = sb("w2_s", [P, E, FH, D])
        b2_s = sb("b2_s", [P, E, D])
        expert_s = sb("expert_s", [P, 3, E])
        c_s = sb("c_s", [P, B])
        silu_s = sb("silu_s", [P, 3, B])
        wmod_s = sb("wmod_s", [P, 6 * D])
        mod_s = sb("mod_s", [B, 6 * D])
        rows_out = sb("rows_out", [B, MODROWS, D])
        mod_tmp = sb("mod_tmp", [B, 3, 2 * D])
        shift_a = sb("shift_a", [P, B])
        scale_a = sb("scale_a", [P, B])
        minus_half = sb("minus_half", [P, LT])
        eps_s = sb("eps_s", [P, LT])
        ones_row = sb("ones_row", [1, P])
        zero_s = sb("zero_s", [P, 2])
        batch_s = sb("batch_s", [P, LT], I32)
        centred1 = sb("centred1", [P, LT, D])
        centred2 = sb("centred2", [P, LT, D])
        pad_tile = sb("pad_tile", [P, ROW])
        x_s = sb("x_s", [P, T, D])
        v_s = sb("v_s", [P, T, D])
        q_stack = [sb(f"q_stack{p}", [P, H, L], BF16) for p in range(2)]
        k_stack = [sb(f"k_stack{p}", [P, H, L], BF16) for p in range(2)]
        bn1 = sb("bn1", [P, LT, 6])
        mv1 = sb("mv1", [P, LT, 2])
        rstd1 = sb("rstd1", [P, 2, LT])
        xhat1 = sb("xhat1", [P, LT, D])
        h_t = sb("h_t", [P, L])
        qk = sb("qk", [P, 2, L])
        rest = sb("rest", [P, 2, L])
        parts = sb("parts", [P, 2, 2, 3, L], BF16)
        neg_max = sb("neg_max", [P, 2, LT * H])
        exp_sum = sb("exp_sum", [P, 2, LT * H])
        att = sb("att", [P, 2, LT * H])
        mod_b = [sb(f"mod_b{p}", [P, MODROWS, D]) for p in range(2)]
        w_gated = sb("w_gated", [P, D])
        opt = sb("opt", [P, LT, D])
        opt_t = sb("opt_t", [P, L])
        bn2 = sb("bn2", [P, LT, 6])
        mv2 = sb("mv2", [P, LT, 2])
        rstd2 = sb("rstd2", [P, 2, LT])
        xhat2 = sb("xhat2", [P, LT, D])
        h_scaled = sb("h_scaled", [P, LT, D])
        h2_t = sb("h2_t", [P, L])
        rows = [sb(f"rows{p}", [P, LT, ROW]) for p in range(2)]
        top = sb("top", [P, LT])
        below = sb("below", [P, LT, E])
        exp_l = sb("exp_l", [P, LT, E])
        first = sb("first", [P, LT, E])
        rank_top = sb("rank_top", [P, LT])
        one_hot = sb("one_hot", [P, LT, E], BF16)
        weight = sb("weight", [P, 2, LT])
        place = sb("place", [P, 2, LT, E])
        place_i = [sb(f"place_i{p}", [P, LT], I32) for p in range(2)]
        next_row = sb("next_row", [P, E])
        token_id = sb("token_id", [P, LT], I32)
        count_f = sb("count_f", [P, 8, E])
        count_i = sb("count_i", [P, 2, E], I32)
        tile_no = sb("tile_no", [NT, 2])
        x_room = x_s[:, :, :].rearrange("p t d -> p (t d)")

        in_expert = sb("in_expert", [NT, 3, E])
        sums_of = sb("sums_of", [NT, 3, E])
        map_p = sb("map_p", [NT, 3, E])
        map_f = sb("map_f", [NT, 5])
        expert_now = sb("expert_now", [1, NT + SLOTS], I32)
        expert_late = sb("expert_late", [1, NT + SLOTS], I32)
        tile_row = sb("tile_row", [1, NT], I32)
        end_row = sb("end_row", [1, 16], I32)
        rows_in = [x_room[:, s * ROW:s * ROW + ROW] for s in range(SLOTS)]
        x_t = sb("x_t", [P, BUFS, P])
        w1_e = sb("w1_e", [P, BUFS, W1X])
        hid = sb("hid", [P, BUFS, FH, P])
        y_biased_s = sb("y_biased_s", [P, 2, D])
        y_gated_s = sb("y_gated_s", [P, 2, D])
        out_s = [v_s[:, s, :] for s in range(SLOTS)]

        scores = ps("scores", [P, RING, HU * L])
        side_a = ps("side_a", [P, 512])
        side_b = ps("side_b", [P, 512])
        xhat_v = side_a[:, 0:L]
        opt_pr = side_a[:, L:2 * L]
        h2_turn = side_b[:, 0:L]
        logit_p = side_b[:, L:L + LT * E]
        rank_p = side_b[:, L + 32:L + 32 + LT * E]
        total_p = side_b[:, L + 64:L + 64 + E]
        hidden = [scores[:, 0, m * 512:m * 512 + F] for m in range(2)]
        expert_out = [scores[:, 1, m * 512:m * 512 + D] for m in range(2)]
        map_out = [side_a[0:1, n * NT:n * NT + NT] for n in range(2)]
        turned = [scores[:, 2, m * 512:m * 512 + P] for m in range(2)]

        c_loaded = sem("c_loaded")
        wmod_loaded = sem("wmod_loaded")
        w_in_loaded = sem("w_in_loaded")
        w_moe_loaded = sem("w_moe_loaded")
        x_loaded = [sem(f"x_loaded{n}") for n in range(len(X_CHUNKS))]
        consts_set = sem("consts_set")
        stacks_set = sem("stacks_set")
        exp_c = sem("exp_c")
        silu_done = sem("silu_done")
        weights_scaled = sem("weights_scaled")
        mod_done = sem("mod_done")
        mod_taken = sem("mod_taken")
        mod_ready = sem("mod_ready")
        mod_stored = sem("mod_stored")
        mod_b_loaded = [sem("mod_b_loaded0"), sem("mod_b_loaded1")]
        pad_set = sem("pad_set")
        pad_stored = sem("pad_stored")
        dve_steps = sem("dve_steps")
        pool_steps = sem("pool_steps")
        dve_held = sem("dve_held")
        sp_held = sem("sp_held")
        pool_held = sem("pool_held")
        stats1 = sem("stats1")
        xhat1_ready = sem("xhat1_ready")
        xhat1_turned = sem("xhat1_turned")
        h_ready = sem("h_ready")
        qk_done = sem("qk_done")
        v_done = sem("v_done")
        qk_ready = sem("qk_ready")
        v_ready = sem("v_ready")
        parts_ready = sem("parts_ready")
        parts_stored = sem("parts_stored")
        stacked = [sem("stacked0"), sem("stacked1")]
        scored = sem("scored")
        maxed = sem("maxed")
        exped = sem("exped")
        att_ready = sem("att_ready")
        gated = sem("gated")
        opt_ready = sem("opt_ready")
        opt_turned = sem("opt_turned")
        opt_t_ready = sem("opt_t_ready")
        projected = sem("projected")
        stats2 = sem("stats2")
        h2_ready = sem("h2_ready")
        h2_turned = sem("h2_turned")
        h2_t_ready = sem("h2_t_ready")
        logits_done = sem("logits_done")
        below_ready = sem("below_ready")
        expl_ready = sem("expl_ready")
        hot_ready = sem("hot_ready")
        ranked = sem("ranked")
        counted = sem("counted")
        placed = sem("placed")
        weighed = sem("weighed")
        weighted = sem("weighted")
        scattered = [sem("scattered0"), sem("scattered1")]
        ends_ready = sem("ends_ready")
        map_set = sem("map_set")
        map_turned = sem("map_turned")
        map_ready = sem("map_ready")
        tails_padded = sem("tails_padded")
        rows_loaded = [sem(f"rows_loaded{s}") for s in range(SLOTS)]
        x_turned = sem("x_turned")
        x_t_ready = sem("x_t_ready")
        w1_ready = sem("w1_ready")
        hid_done = sem("hid_done")
        hid_ready = sem("hid_ready")
        y_done = sem("y_done")
        y_biased = sem("y_biased")
        y_gated = sem("y_gated")
        out_ready = sem("out_ready")
        out_stored = [sem(f"out_stored{s}") for s in range(SLOTS)]

        LOADS_IN = 12
        SETS = 6

        block = ctx.enter_context(nc.Block())

        def load_many(eng, row, at, n, low, high):
            return nc.values_load_multi_w_load_instructions(
                row[0:1, ds(at, n)], (eng.engine,), min_val=low, max_val=high,
                skip_runtime_bounds_check_because="counts and experts are bounded by the shapes")[1]

        def split_by(eng, steps, b, p):
            eng.wait_ge(qk_ready, b + 1)
            need(eng, parts_stored, 16 * b - 16)
            zeros = zero_s[:, :].rearrange("p (s o) -> p s o", o=1).broadcast_to([P, 2, L])
            steps.then(eng.tensor_tensor(parts[:, p, :, 0, :], qk[:, :, :], zeros, ALU.add))
            steps.then(eng.tensor_tensor(rest[:, :, :], qk[:, :, :], parts[:, p, :, 0, :], ALU.subtract))
            steps.then(eng.tensor_tensor(parts[:, p, :, 1, :], rest[:, :, :], zeros, ALU.add))
            eng.tensor_tensor(parts[:, p, :, 2, :], rest[:, :, :], parts[:, p, :, 1, :], ALU.subtract).then_inc(parts_ready, 1)

        def load_stacks_by(eng, p, sides):
            for n in range(COMBOS):
                r = slice(DH * n, DH * n + DH)
                for side in sides:
                    to, part = ((q_stack, Q_PART), (k_stack, K_PART))[side]
                    eng.dma_start(to[p][r, :, :], parts_dram[p, side, part[n]].rearrange("(h d) t -> d h t", d=DH)).then_inc(stacked[p], 16)

        @block.sync
        def _(sp):
            steps = Steps(sp, sp_held, sp_held)
            sp.dma_start(c_s[:, :], c_t).then_inc(c_loaded, 16)

            def load_x(n):
                t = slice(LT * X_CHUNKS[n][0], LT * X_CHUNKS[n][1])
                sp.dma_start(x_s[:, t, :], x_tiles[:, t, :]).then_inc(x_loaded[n], 16)

            load_x(0)
            sp.dma_start(wmod_s[:, :], wmod).then_inc(wmod_loaded, 16)
            load_x(1)
            sp.dma_start(ident_s[:, :], ident).then_inc(w_in_loaded, 16)
            sp.dma_start(w_qkv_s[:, :, :], w_qkv).then_inc(w_in_loaded, 16)
            sp.dma_start(b_qk_s[:, :], b_qk).then_inc(w_in_loaded, 16)
            sp.dma_start(b_v_s[:, :], b_v.broadcast_to([P, D])).then_inc(w_in_loaded, 16)
            sp.dma_start(w_out_s[:, :], w_out).then_inc(w_in_loaded, 16)
            sp.dma_start(b_out_s[:, :], b_out.broadcast_to([B, D])).then_inc(w_in_loaded, 16)
            sp.dma_start(router_s[:, :], router_w).then_inc(w_in_loaded, 16)
            sp.dma_start(before_f[:, :], before).then_inc(w_in_loaded, 16)
            sp.dma_start(expert_s[:, :, :], expert_row.broadcast_to([P, 3 * E])).then_inc(w_in_loaded, 16)
            sp.dma_start(tile_no[:, :], tile_numbers).then_inc(w_in_loaded, 16)
            sp.dma_start(token_id[:, :], token_numbers).then_inc(w_in_loaded, 16)
            sp.dma_start(next_row[:, :], first_row.broadcast_to([P, E])).then_inc(w_in_loaded, 16)
            load_x(2)
            load_x(3)
            sp.wait_ge(pad_set, 2)
            sp.dma_start(table[PAD_AT:PAD_AT + P, :], pad_tile[:, :]).then_inc(pad_stored, 16)

            def store_parts(b, p):
                sp.wait_ge(parts_ready, b + 1)
                sp.dma_start(parts_dram[p].rearrange("q s r t -> r (q s) t"),
                             parts[:, p].rearrange("r q s t -> r (q s) t")).then_inc(parts_stored, 16)
                sp.wait_ge(parts_stored, 16 * b + 16)
                steps.plain()

            def load_stacks(b, p, sides=(0, 1)):
                load_stacks_by(sp, p, sides)

            sp.wait_ge(stacks_set, 4)
            for b in range(2):
                store_parts(b, b)
                if b == 0:
                    load_stacks(b, b, (0,))
                    sp.wait_ge(mod_ready, 1)
                    sp.dma_start(mod_rows, rows_out[:, :, :].rearrange("b r d -> b (r d)")).then_inc(mod_stored, 16)
                else:
                    load_stacks(b, b)
            sp.wait_ge(mod_stored, 16)
            sp.dma_start(w1x_s[:, :, :], w1x).then_inc(w_moe_loaded, 16)
            sp.dma_start(w2_s[:, :, :, :], w2).then_inc(w_moe_loaded, 16)
            sp.dma_start(b2_s[:, :, :], b2.broadcast_to([P, E * D])).then_inc(w_moe_loaded, 16)

            def iteration(b, p):
                need(sp, weighted, b - 1)
                sp.dma_start(mod_b[p][:, :, :], mod_rows[ds(b, 1), :].broadcast_to([P, MODROWS * D])).then_inc(mod_b_loaded[p], 16)
                if has_prep(b):
                    store_parts(b + 2, p)
                if has_prep(b):
                    sp.wait_ge(scored, UNITS * b + UNITS)
                    load_stacks(b + 2, p)

            over_batches(sp, iteration, lambda b, p: None)

            sp.wait_ge(ends_ready, 1)
            sp.wait_ge(pad_stored, 16)
            ends = load_many(sp, end_row, 0, E, 0, E * ROOM)
            for e in range(E):
                sp.dma_start(table[ds(ends[e], P), :], pad_tile[:, :]).then_inc(tails_padded, 16)
            sp.wait_ge(scattered[0], 16 * T // 2)
            sp.wait_ge(scattered[1], 16 * T // 2)
            sp.wait_ge(tails_padded, 16 * E)
            sp.wait_ge(map_ready, 1)

            def load(j, s, turn):
                if s == 0:
                    rows_of_turn[:] = load_many(sp, tile_row, SLOTS * turn, SLOTS, 0, PAD_AT)
                need(sp, out_stored[s], 16 * turn)
                sp.dma_start(rows_in[s][:, :], table[ds(rows_of_turn[s], P), :]).then_inc(rows_loaded[s], 16)

            rows_of_turn = []
            over_tiles(sp, load, 0)
            for s in range(SLOTS):
                sp.wait_ge(out_stored[s], 16 * NT // SLOTS)

        @block.gpsimd
        def _(pool):
            steps = Steps(pool, pool_steps, pool_held)
            pool.memset(ones_s[:, :], 1.0).then_inc(consts_set, 1)
            pool.memset(minus_half[:, :], -0.5).then_inc(consts_set, 1)
            pool.memset(eps_s[:, :], EPS).then_inc(consts_set, 1)
            pool.memset(zero_s[:, :], 0.0).then_inc(consts_set, 1)
            pool.memset(ones_row[:, :], 1.0).then_inc(consts_set, 1)
            pool.memset(batch_s[:, :], L).then_inc(consts_set, 1)
            pool.memset(pad_tile[:, 0:ID], 0.0).then_inc(pad_set, 1)
            pool.memset(pad_tile[:, ID:ROW].bitcast(I32), int(NO_TOKEN)).then_inc(pad_set, 1)
            pool.wait_ge(consts_set, SETS)

            def normalise(mv, rstd, centred, src, dst):
                def by_token(v):
                    return v.rearrange("p (t o) -> p t o", o=1).broadcast_to([P, LT, D])

                pool.tensor_tensor(centred[:, :, :], src, mv[:, :, 0:1].broadcast_to([P, LT, D]), ALU.subtract)
                steps.then(pool.tensor_tensor(rstd[:, 0, :], mv[:, :, 1], eps_s[:, :], ALU.add))
                steps.then(pool.tensor_tensor(rstd[:, 1, :], rstd[:, 0, :], minus_half[:, :], ALU.pow))
                return pool.tensor_tensor(dst[:, :, :], centred[:, :, :], by_token(rstd[:, 1, :]), ALU.mult)

            def norm_x(b):
                pool.wait_ge(stats1, b + 1)
                need(pool, xhat1_ready, b)
                need(pool, xhat1_turned, b)
                normalise(mv1, rstd1, centred1, x_s[:, ds(LT * b, LT), :], xhat1).then_inc(xhat1_ready, 1)

            def split(b, p):
                split_by(pool, steps, b, p)

            def gate(b, p):
                pool.wait_ge(mod_b_loaded[p], 8 * (b - p) + 16)
                need(pool, projected, b)
                pool.tensor_tensor(w_gated[:, :], w_out_s[:, :], mod_b[p][:, 0, :], ALU.mult).then_inc(gated, 1)

            def attend(b, p):
                pool.wait_ge(att_ready, b + 1)
                need(pool, opt_turned, b)
                for t in range(LT):
                    last = pool.tensor_tensor(
                        opt[:, t, :].rearrange("p (h d) -> p h d", d=DH),
                        v_s[:, ds(LT * b + t, 1), :].rearrange("p t (h d) -> p (t h) d", d=DH),
                        att[:, 1, t * H:t * H + H].rearrange("p (h o) -> p h o", o=1).broadcast_to([P, H, DH]),
                        ALU.mult)
                last.then_inc(opt_ready, 1)

            def norm_x2(b, p):
                pool.wait_ge(stats2, b + 1)
                need(pool, scattered[p], 8 * LT * (b - p))
                steps.then(normalise(mv2, rstd2, centred2, rows[p][:, :, X2:X2 + D], xhat2))
                steps.then(pool.tensor_tensor(h_scaled[:, :, :], xhat2[:, :, :],
                                              mod_b[p][:, 2:3, :].broadcast_to([P, LT, D]), ALU.mult))
                pool.tensor_tensor(rows[p][:, :, H2:H2 + D], h_scaled[:, :, :],
                                   mod_b[p][:, 3:4, :].broadcast_to([P, LT, D]), ALU.add).then_inc(h2_ready, 1)

            def scatter(b, p):
                pool.wait_ge(placed, b + 1)
                pool.wait_ge(weighed, b + 1)
                pool.tensor_tensor(rows[p][:, :, ID:ROW].bitcast(I32), token_id[:, :].rearrange("p (t o) -> p t o", o=1),
                                   batch_s[:, :].rearrange("p (t o) -> p t o", o=1), ALU.add)
                steps.then(pool.tensor_tensor(token_id[:, :], token_id[:, :], batch_s[:, :], ALU.add))
                pool.tensor_tensor(rows[p][:, :, GW:GW + D], mod_b[p][:, 4:5, :].broadcast_to([P, LT, D]),
                                   weight[:, 1, :].rearrange("p (t o) -> p t o", o=1).broadcast_to([P, LT, D]),
                                   ALU.mult).then_inc(weighted, 1)
                pool.wait_ge(weighted, b + 1)
                steps.plain()
                for t in range(LT):
                    pool.indirect_dma_start(table, bass.IndirectOffsetOnAxis(ap=place_i[p][:, t:t + 1], axis=0),
                                            rows[p][:, t, :], None).then_inc(scattered[p], 16)

            for b in range(3):
                norm_x(b)
            pool.wait_ge(w_in_loaded, 16 * LOADS_IN)

            def iteration(b, p):
                if has_tail(b):
                    attend(b - 1, 1 - p)
                if has_tail(b):
                    gate(b - 1, 1 - p)
                if has_norm(b):
                    norm_x(b + 3)
                if has_routing(b):
                    scatter(b - 2, p)
                if has_tail(b):
                    norm_x2(b - 1, 1 - p)
                if has_prep(b):
                    split(b + 2, p)

            def drain(b, p):
                attend(b - 1, 1 - p)
                gate(b - 1, 1 - p)
                norm_x2(b - 1, 1 - p)
                scatter(b - 2, p)
                scatter(b - 1, 1 - p)

            over_batches(pool, iteration, drain, steps, TURN * STEPS_POOL)

            def store(j, s, turn):
                pool.wait_ge(out_ready, j + 1)
                steps.plain()
                pool.indirect_dma_start(out_rows, bass.IndirectOffsetOnAxis(ap=rows_in[s][:, ID:ROW].bitcast(I32), axis=0),
                                        out_s[s][:, :], None, bounds_check=NTOK - 1, oob_is_err=False).then_inc(out_stored[s], 16)

            over_tiles(pool, store, 0)

        @block.scalar
        def _(act):
            act.wait_ge(c_loaded, 16)
            act.activation(silu_s[:, 0, :], c_s[:, :], ACT.Exp, scale=-1.0).then_inc(exp_c, 1)

            def iteration(b, p):
                for u in range(UNITS):
                    act.wait_ge(maxed, UNITS * b + u + 1)
                    buf = scores[:, u % RING, :]
                    for k in range(UNIT[u]):
                        n = START[u] + k
                        last = act.activation(buf[:, k * L:k * L + L], buf[:, k * L:k * L + L], ACT.Exp,
                                              bias=neg_max[:, p, n:n + 1], accum_out=exp_sum[:, p, n:n + 1])
                    last.then_inc(exped, 1)
                    if u == 3 and has_routing(b):
                        router_exp(b - 2)
                    if u == 3 and has_tail(b):
                        take_opt(b - 1)

            def take_opt(b):
                act.wait_ge(opt_turned, b + 1)
                act.copy(opt_t[:, :], opt_pr).then_inc(opt_t_ready, 1)

            def router_exp(b):
                act.wait_ge(below_ready, b + 1)
                act.activation(exp_l[:, :, :], below[:, :, :], ACT.Exp).then_inc(expl_ready, 1)

            def drain(b, p):
                take_opt(b - 1)
                router_exp(b - 2)
                router_exp(b - 1)

            act.wait_ge(parts_stored, 16)
            act.wait_ge(stacks_set, 4)
            load_stacks_by(act, 0, (1,))
            over_batches(act, iteration, drain)

            def gelu(j, s, turn):
                if in_range(j):
                    act.wait_ge(x_turned, j + 1)
                    need(act, hid_done, j - BUFS + 1)
                    act.copy(x_t[:, s % BUFS, :], turned[s % 2]).then_inc(x_t_ready, 1)
                if in_range(j - AT_W1):
                    n, k = j - AT_W1, (s - AT_W1) % SLOTS
                    act.wait_ge(hid_done, n + 1)
                    need(act, y_done, n - BUFS + 1)
                    for f in range(FH):
                        last = act.activation(hid[:, k % BUFS, f, :], hidden[k % 2][:, f * P:f * P + P], ACT.Gelu,
                                              bias=w1_e[:, k % BUFS, F + f:F + f + 1])
                    last.then_inc(hid_ready, 1)

            over_tiles(act, gelu, AT_W1)

        @block.tensor
        def _(pe):
            pe.wait_ge(silu_done, 1)
            pe.wait_ge(wmod_loaded, 16)
            silu = silu_s[:, 2, :]
            for n in range(2):
                last = pe.matmul(scores[:, 1, n * 512:n * 512 + B], wmod_s[:, n * D:n * D + D], silu, start=True, stop=True)
            last.then_inc(mod_done, 1)
            for n in range(2):
                last = pe.matmul(scores[0:B, 0, n * 512:n * 512 + 3 * D], silu, wmod_s[:, n * 3 * D:(n + 1) * 3 * D], start=True, stop=True)
            last.then_inc(mod_done, 1)

            def turn_x(b):
                pe.wait_ge(xhat1_ready, b + 1)
                need(pe, v_ready, b)
                need(pe, stats2, b - 3)
                for t in range(LT):
                    last = pe.transpose(xhat_v[:, t * P:t * P + P], xhat1[:, t, :], ident_s[:, :])
                last.then_inc(xhat1_turned, 1)

            def project_v(b):
                pe.wait_ge(h_ready, b + 1)
                for t in range(LT):
                    last = pe.matmul(xhat_v[:, t * P:t * P + P], h_t[:, t * P:t * P + P], w_qkv_s[:, 2, :], start=True, stop=True)
                last.then_inc(v_done, 1)

            def project_qk(b):
                need(pe, counted, b - 3)
                need(pe, qk_ready, b)
                for n in range(2):
                    last = pe.matmul(side_b[:, n * L:n * L + L], w_qkv_s[:, n, :], h_t[:, :], start=True, stop=True)
                last.then_inc(qk_done, 1)

            def score(b, p, u):
                if u == 0:
                    pe.wait_ge(stacked[p], (2 * 16 * COMBOS // 2) * (b - p) + 2 * 16 * COMBOS)
                need(pe, exped, UNITS * b + u - RING + 1)
                for k in range(UNIT[u]):
                    t, h = (START[u] + k) // H, (START[u] + k) % H
                    last = pe.matmul(scores[:, u % RING, k * L:k * L + L], q_stack[p][:, h, t * P:t * P + P],
                                     k_stack[p][:, h, :], start=True, stop=True)
                last.then_inc(scored, 1)

            def turn_opt(b, ahead):
                pe.wait_ge(opt_ready, b + 1)
                need(pe, stats2, b)
                pe.wait_ge(v_ready, ahead)
                for t in range(LT):
                    last = pe.transpose(opt_pr[:, t * P:t * P + P], opt[:, t, :], ident_s[:, :])
                last.then_inc(opt_turned, 1)

            def project_out(b, p):
                pe.wait_ge(opt_t_ready, b + 1)
                pe.wait_ge(gated, b + 1)
                for t in range(LT):
                    pe.matmul(opt_pr[:, t * P:t * P + P], opt_t[:, t * P:t * P + P], w_gated[:, :], start=True, stop=False)
                    last = pe.matmul(opt_pr[:, t * P:t * P + P], ones_row[:, :], mod_b[p][0:1, 1, :], start=False, stop=True)
                last.then_inc(projected, 1)

            def turn_h2(b, p, ahead):
                pe.wait_ge(h2_ready, b + 1)
                need(pe, counted, b)
                pe.wait_ge(qk_ready, ahead)
                for t in range(LT):
                    last = pe.transpose(h2_turn[:, t * P:t * P + P], rows[p][:, t, H2:H2 + D], ident_s[:, :])
                last.then_inc(h2_turned, 1)

            def route(b):
                pe.wait_ge(h2_t_ready, b + 1)
                for t in range(LT):
                    last = pe.matmul(logit_p[:, t * E:t * E + E], h2_t[:, t * P:t * P + P], router_s[:, :], start=True, stop=True)
                last.then_inc(logits_done, 1)

            def rank(b):
                pe.wait_ge(hot_ready, b + 1)
                pe.matmul(rank_p[:, 0:E], before_s[:, :], one_hot[:, 0, :], start=True, stop=True)
                pe.matmul(rank_p[:, E:2 * E], before_s[:, :], one_hot[:, 1, :], start=True, stop=False)
                pe.matmul(rank_p[:, E:2 * E], ones_s[:, :], one_hot[:, 0, :], start=False, stop=True)
                pe.matmul(total_p, ones_s[:, :], one_hot[:, 0, :], start=True, stop=False)
                pe.matmul(total_p, ones_s[:, :], one_hot[:, 1, :], start=False, stop=True).then_inc(ranked, 1)

            pe.wait_ge(w_in_loaded, 16 * LOADS_IN)
            pe.wait_ge(weights_scaled, 3)
            for b in range(2):
                turn_x(b)
                project_v(b)
                project_qk(b)
            pe.wait_ge(mod_taken, 2)

            def up_to(b):
                return min(b, B) if isinstance(b, int) else b

            def iteration(b, p):
                score(b, p, 0)
                if has_prep(b):
                    turn_x(b + 2)
                score(b, p, 1)
                if has_routing(b):
                    turn_h2(b - 2, p, up_to(b + 2))
                score(b, p, 2)
                score(b, p, 3)
                if has_prep(b):
                    project_v(b + 2)
                if has_routing(b):
                    route(b - 2)
                score(b, p, 4)
                if has_tail(b):
                    turn_opt(b - 1, up_to(b + 3))
                score(b, p, 5)
                if has_routing(b):
                    rank(b - 2)
                score(b, p, 6)
                if has_tail(b):
                    project_out(b - 1, 1 - p)
                score(b, p, 7)
                if has_prep(b):
                    project_qk(b + 2)
                score(b, p, 8)

            def drain(b, p):
                turn_h2(b - 2, p, B)
                turn_opt(b - 1, B)
                route(b - 2)
                project_out(b - 1, 1 - p)
                rank(b - 2)
                turn_h2(b - 1, 1 - p, B)
                route(b - 1)
                rank(b - 1)

            over_batches(pe, iteration, drain)

            pe.wait_ge(map_set, 1)
            for n in range(2):
                last = pe.matmul(map_out[n], map_f[:, 3 + n:4 + n], ident_s[0:NT, 0:NT], start=True, stop=True)
            last.then_inc(map_turned, 1)
            pe.wait_ge(map_ready, 1)
            pe.wait_ge(w_moe_loaded, 48)
            experts = []

            def tile(j, s, turn):
                if s == 0:
                    experts[:] = load_many(pe, expert_late, SLOTS * turn, SLOTS, 0, E - 1)
                if in_range(j):
                    pe.wait_ge(rows_loaded[s], 16 * turn + 16)
                    need(pe, x_t_ready, j - 1)
                    pe.transpose(turned[s % 2], rows_in[s][:, H2:H2 + D], ident_s[:, :]).then_inc(x_turned, 1)
                if in_range(j - AT_W1):
                    n, k = j - AT_W1, (s - AT_W1) % SLOTS
                    pe.wait_ge(x_t_ready, n + 1)
                    pe.wait_ge(w1_ready, n + 1)
                    need(pe, hid_ready, n - 1)
                    for f in range(FH):
                        last = pe.matmul(hidden[k % 2][:, f * P:f * P + P], w1_e[:, k % BUFS, f * P:f * P + P],
                                         x_t[:, k % BUFS, :], start=True, stop=True)
                    last.then_inc(hid_done, 1)
                if in_range(j - AT_W2):
                    n, k = j - AT_W2, (s - AT_W2) % SLOTS
                    pe.wait_ge(hid_ready, n + 1)
                    need(pe, y_biased, n - 1)
                    for f in range(FH):
                        last = pe.matmul(expert_out[k % 2], hid[:, k % BUFS, f, :], w2_s[:, ds(experts[s], 1), f, :],
                                         start=(f == 0), stop=(f == FH - 1))
                    last.then_inc(y_done, 1)

            over_tiles(pe, tile, AT_W2)

        @block.vector
        def _(dve):
            steps = Steps(dve, dve_steps, dve_held)
            for p in range(2):
                dve.memset(q_stack[p][:, :, :], 0.0).then_inc(stacks_set, 1)
                dve.memset(k_stack[p][:, :, :], 0.0).then_inc(stacks_set, 1)
            dve.wait_ge(exp_c, 1)
            steps.then(dve.tensor_scalar(silu_s[:, 0, :], silu_s[:, 0, :], 1.0, None, ALU.add))
            steps.then(dve.reciprocal(silu_s[:, 1, :], silu_s[:, 0, :]))
            dve.tensor_tensor(silu_s[:, 2, :], c_s[:, :], silu_s[:, 1, :], ALU.mult).then_inc(silu_done, 1)
            step = {}

            def sums_of_rows(src, bn, key):
                for t in range(LT):
                    last = dve.bn_stats(bn[:, t, :], src(t))
                step[key] = steps.did(last)

            def aggregate(bn, mv, key):
                steps.after(step[key], plain=True)
                for t in range(LT):
                    last = dve.bn_aggr(mv[:, t, :], bn[:, t, :])
                return last

            def stats_x(b, p):
                if isinstance(b, int):
                    dve.wait_ge(x_loaded[next(n for n, c in enumerate(X_CHUNKS) if c[0] <= b < c[1])], 16)
                need(dve, stats1, b)
                sums_of_rows(lambda t: x_s[:, ds(LT * b + t, 1), :].rearrange("p t d -> p (t d)"), bn1, "x")

            def mean_x(b):
                need(dve, xhat1_ready, b)
                aggregate(bn1, mv1, "x").then_inc(stats1, 1)

            def make_h(b):
                dve.wait_ge(xhat1_turned, b + 1)
                dve.tensor_scalar(h_t[:, :], xhat_v, scale_a[:, ds(b, 1)], shift_a[:, ds(b, 1)], ALU.mult, ALU.add).then_inc(h_ready, 1)

            def take_qk(b):
                dve.wait_ge(qk_done, b + 1)
                need(dve, parts_ready, b)
                dve.tensor_tensor(qk[:, :, :], side_b[:, :].rearrange("p (s t) -> p s t", s=2),
                                  b_qk_s[:, :].rearrange("p (s o) -> p s o", o=1).broadcast_to([P, 2, L]), ALU.add).then_inc(qk_ready, 1)

            def take_v(b):
                dve.wait_ge(v_done, b + 1)
                dve.tensor_tensor(v_s[:, ds(LT * b, LT), :], xhat_v.rearrange("p (t d) -> p t d", t=LT),
                                  b_v_s[:, :].rearrange("p (o d) -> p o d", o=1).broadcast_to([P, LT, D]), ALU.add).then_inc(v_ready, 1)

            def row_max(b, p, u):
                dve.wait_ge(scored, UNITS * b + u + 1)
                dve.tensor_reduce(neg_max[:, p, START[u]:START[u] + UNIT[u]],
                                  scores[:, u % RING, 0:UNIT[u] * L].rearrange("p (h m) -> p h m", m=L),
                                  AX_X, ALU.max, negate=True).then_inc(maxed, 1)

            def attention_sums(b, p):
                dve.wait_ge(exped, UNITS * b + UNITS)
                need(dve, att_ready, b)
                step["att"] = steps.did(dve.reciprocal(att[:, 0, :], exp_sum[:, p, :]))

            def attention_rows(b, p):
                need(dve, opt_ready, b)
                steps.after(step["att"])
                dve.tensor_tensor(att[:, 1, :], exp_sum[:, p, :], att[:, 0, :], ALU.mult).then_inc(att_ready, 1)

            def residual(b, p):
                dve.wait_ge(projected, b + 1)
                need(dve, scattered[p], 8 * LT * (b - p))
                step["x2"] = steps.did(dve.tensor_tensor(rows[p][:, :, X2:X2 + D], opt_pr.rearrange("p (t d) -> p t d", t=LT),
                                             x_s[:, ds(LT * b, LT), :], ALU.add))

            def stats_x2(b, p):
                need(dve, stats2, b)
                steps.after(step["x2"], plain=True)
                sums_of_rows(lambda t: rows[p][:, t, X2:X2 + D], bn2, "rows")

            def mean_x2(b):
                need(dve, h2_ready, b)
                aggregate(bn2, mv2, "rows").then_inc(stats2, 1)

            def take_h2(b):
                dve.wait_ge(h2_turned, b + 1)
                dve.tensor_copy(h2_t[:, :], h2_turn).then_inc(h2_t_ready, 1)

            def bcast(v):
                return v.rearrange("p (t o) -> p t o", o=1).broadcast_to([P, LT, E])

            def per_tile(v):
                return v.rearrange("p (o e) -> p o e", o=1).broadcast_to([P, LT, E])

            logits = logit_p.rearrange("p (t e) -> p t e", t=LT)

            def highest(b):
                dve.wait_ge(logits_done, b + 1)
                need(dve, below_ready, b)
                step["top"] = steps.did(dve.tensor_reduce(top[:, :], logits, AX_X, ALU.max))

            def compare(b):
                steps.after(step["top"])
                dve.tensor_tensor(below[:, :, :], logits, bcast(top[:, :]), ALU.subtract).then_inc(below_ready, 1)

            def candidates(b):
                dve.wait_ge(below_ready, b + 1)
                need(dve, hot_ready, b)
                step["first"] = steps.did(dve.scalar_tensor_tensor(out=first[:, :, :], in0=below[:, :, :], scalar=0.0,
                                                    in1=per_tile(expert_s[:, 0, :]), op0=ALU.is_ge, op1=ALU.mult))

            def choose(b):
                steps.after(step["first"])
                step["rank"] = steps.did(dve.tensor_reduce(rank_top[:, :], first[:, :, :], AX_X, ALU.max))

            def mark(b):
                steps.after(step["rank"])
                dve.tensor_tensor(one_hot[:, :, :], first[:, :, :], bcast(rank_top[:, :]), ALU.is_equal).then_inc(hot_ready, 1)

            def find_place(b, p):
                dve.wait_ge(ranked, b + 1)
                need(dve, placed, b)
                step["place"] = steps.did(dve.tensor_tensor(place[:, 0], rank_p.rearrange("p (t e) -> p t e", t=LT), per_tile(next_row[:, :]), ALU.add))

            def own_place(b):
                steps.after(step["place"])
                dve.tensor_tensor(next_row[:, :], next_row[:, :], total_p, ALU.add).then_inc(counted, 1)
                step["own"] = steps.did(dve.tensor_tensor(place[:, 1], place[:, 0], one_hot[:, :, :], ALU.mult))

            def note_place(b, p):
                steps.after(step["own"])
                dve.tensor_reduce(place_i[p][:, :], place[:, 1], AX_X, ALU.max).then_inc(placed, 1)

            def weigh(b):
                dve.wait_ge(expl_ready, b + 1)
                need(dve, weighed, b)
                step["weight"] = steps.did(dve.tensor_reduce(weight[:, 0, :], exp_l[:, :, :], AX_X, ALU.add))

            def invert_weight(b):
                steps.after(step["weight"])
                need(dve, weighted, b)
                dve.reciprocal(weight[:, 1, :], weight[:, 0, :]).then_inc(weighed, 1)

            for b in range(2):
                stats_x(b, b)
                mean_x(b)
            dve.wait_ge(w_in_loaded, 16 * LOADS_IN)
            dve.tensor_copy(before_s[:, :], before_f[:, :]).then_inc(weights_scaled, 1)
            dve.tensor_scalar(b_qk_s[:, 0:1], b_qk_s[:, 0:1], SCALE, None, ALU.mult).then_inc(weights_scaled, 1)
            dve.tensor_scalar(w_qkv_s[:, 0, :], w_qkv_s[:, 0, :], SCALE, None, ALU.mult).then_inc(weights_scaled, 1)
            dve.wait_ge(weights_scaled, 3)
            dve.wait_ge(mod_done, 1)
            dve.tensor_copy(shift_a[:, :], scores[:, 1, 0:B])
            steps.then(dve.tensor_scalar(scale_a[:, :], scores[:, 1, 512:512 + B], 1.0, None, ALU.add))
            dve.wait_ge(consts_set, SETS)

            def modulate():
                dve.wait_ge(mod_done, 2)
                for n in range(2):
                    dve.tensor_copy(mod_s[:, n * 3 * D:(n + 1) * 3 * D], scores[0:B, 0, n * 512:n * 512 + 3 * D]).then_inc(mod_taken, 1)
                dve.wait_ge(mod_taken, 2)
                for n, chunk in enumerate((2, 5)):
                    g = mod_s[:, chunk * D:chunk * D + D]
                    w = slice(n * D, n * D + D)
                    steps.then(dve.tensor_scalar(mod_tmp[:, 0, w], g, 0.0, 2.0, ALU.is_ge, ALU.mult))
                    steps.then(dve.tensor_scalar(mod_tmp[:, 1, w], g, -1.0, None, ALU.mult))
                    steps.then(dve.tensor_tensor(mod_tmp[:, 2, w], mod_tmp[:, 1, w], g, ALU.max))
                    steps.then(dve.tensor_scalar(mod_tmp[:, 1, w], mod_tmp[:, 2, w], 0.25, None, ALU.max))
                    steps.then(dve.tensor_scalar(mod_tmp[:, 2, w], mod_tmp[:, 0, w], -1.0, None, ALU.add))
                    steps.then(dve.tensor_tensor(rows_out[:, (0, 4)[n], :], mod_tmp[:, 1, w], mod_tmp[:, 2, w], ALU.mult))
                dve.tensor_tensor(rows_out[:, 1, :], rows_out[:, 0, :], b_out_s[:, :], ALU.mult)
                dve.tensor_scalar(rows_out[:, 2, :], mod_s[:, 4 * D:5 * D], 1.0, None, ALU.add)
                dve.tensor_copy(rows_out[:, 3, :], mod_s[:, 3 * D:4 * D]).then_inc(mod_ready, 1)

            for b in range(2):
                make_h(b)
                take_v(b)
                take_qk(b)
                split_by(dve, steps, b, b)
            stats_x(2, 0)
            mean_x(2)
            modulate()

            def iteration(b, p):
                row_max(b, p, 0)
                if has_prep(b):
                    make_h(b + 2)
                if has_norm(b):
                    stats_x(b + 3, 1 - p)
                row_max(b, p, 1)
                if has_tail(b):
                    attention_sums(b - 1, 1 - p)
                if has_routing(b):
                    take_h2(b - 2)
                if has_tail(b):
                    attention_rows(b - 1, 1 - p)
                row_max(b, p, 2)
                if has_prep(b):
                    take_v(b + 2)
                row_max(b, p, 3)
                if has_routing(b):
                    highest(b - 2)
                row_max(b, p, 4)
                if has_routing(b):
                    compare(b - 2)
                if has_norm(b):
                    mean_x(b + 3)
                if has_routing(b):
                    candidates(b - 2)
                if has_routing(b):
                    choose(b - 2)
                if has_routing(b):
                    mark(b - 2)
                row_max(b, p, 5)
                if has_routing(b):
                    find_place(b - 2, p)
                if has_routing(b):
                    weigh(b - 2)
                if has_routing(b):
                    own_place(b - 2)
                if has_routing(b):
                    note_place(b - 2, p)
                if has_routing(b):
                    invert_weight(b - 2)
                row_max(b, p, 6)
                if has_tail(b):
                    residual(b - 1, 1 - p)
                if has_tail(b):
                    stats_x2(b - 1, 1 - p)
                if has_tail(b):
                    mean_x2(b - 1)
                row_max(b, p, 7)
                if has_prep(b):
                    take_qk(b + 2)
                row_max(b, p, 8)

            def drain(b, p):
                attention_sums(b - 1, 1 - p)
                take_h2(b - 2)
                attention_rows(b - 1, 1 - p)
                highest(b - 2)
                compare(b - 2)
                candidates(b - 2)
                choose(b - 2)
                mark(b - 2)
                residual(b - 1, 1 - p)
                stats_x2(b - 1, 1 - p)
                mean_x2(b - 1)
                find_place(b - 2, p)
                weigh(b - 2)
                own_place(b - 2)
                note_place(b - 2, p)
                invert_weight(b - 2)
                take_h2(b - 1)
                highest(b - 1)
                compare(b - 1)
                candidates(b - 1)
                choose(b - 1)
                mark(b - 1)
                find_place(b - 1, 1 - p)
                weigh(b - 1)
                own_place(b - 1)
                note_place(b - 1, 1 - p)
                invert_weight(b - 1)

            over_batches(dve, iteration, drain, steps, TURN * STEPS_DVE, lambda: dve.wait_ge(x_loaded[3], 16))

            first_e = expert_s[:, 2, :]
            dve.wait_ge(counted, B)
            dve.tensor_copy(end_row[:, 0:E], next_row[0:1, :]).then_inc(ends_ready, 1)
            steps.then(dve.tensor_tensor(count_f[:, 0, :], next_row[:, :], first_e, ALU.subtract))
            steps.then(dve.tensor_scalar(count_i[:, 0, :], count_f[:, 0, :], float(P - 1), None, ALU.add))
            steps.then(dve.tensor_scalar(count_i[:, 1, :], count_i[:, 0, :], P.bit_length() - 1, None, ALU.arith_shift_right))
            steps.then(dve.tensor_copy(count_f[:, 2, :], count_i[:, 1, :]))
            at, shift = 2, 1
            while shift < E:
                to = {2: 3, 3: 4, 4: 3}[at]
                dve.tensor_copy(count_f[:, to, 0:shift], count_f[:, at, 0:shift])
                steps.then(dve.tensor_tensor(count_f[:, to, shift:E], count_f[:, at, shift:E], count_f[:, at, 0:E - shift], ALU.add))
                at, shift = to, 2 * shift
            steps.then(dve.tensor_tensor(count_f[:, 5, :], count_f[:, at, :], count_f[:, 2, :], ALU.subtract))
            steps.then(dve.tensor_scalar(count_f[:, 6, :], count_f[:, 5, :], -float(P), None, ALU.mult))
            dve.tensor_tensor(sums_of[:, 2, :], count_f[0:NT, 6, :], first_e[0:NT], ALU.add)
            dve.memset(sums_of[:, 0, :], 1.0)
            dve.tensor_copy(sums_of[:, 1, :], expert_s[0:NT, 1, :])
            tile = tile_no[:, 1:2].broadcast_to([NT, E])
            dve.tensor_tensor(in_expert[:, 0, :], tile, count_f[0:NT, 5, :], ALU.is_ge)
            steps.then(dve.tensor_tensor(in_expert[:, 1, :], tile, count_f[0:NT, at, :], ALU.is_ge))
            steps.then(dve.tensor_tensor(in_expert[:, 2, :], in_expert[:, 0, :], in_expert[:, 1, :], ALU.subtract))
            steps.then(dve.tensor_tensor(map_p[:, :, :], in_expert[:, 2:3, :].broadcast_to([NT, 3, E]), sums_of[:, :, :], ALU.mult))
            steps.then(dve.tensor_reduce(map_f[:, 0:3], map_p[:, :, :], AX_X, ALU.add))
            dve.tensor_copy(map_f[:, 3:4], map_f[:, 1:2])
            steps.then(dve.tensor_tensor(map_p[:, 0, 0:1], tile_no[:, 0:1], map_f[:, 0:1], ALU.mult))
            dve.tensor_tensor(map_f[:, 4:5], map_p[:, 0, 0:1], map_f[:, 2:3], ALU.add).then_inc(map_set, 1)
            for v in (expert_now, expert_late):
                steps.then(dve.memset(v[:, :], 0))
            dve.wait_ge(map_turned, 1)
            dve.tensor_copy(expert_now[:, 0:NT], map_out[0])
            dve.tensor_copy(expert_late[:, AT_W2:NT + AT_W2], map_out[0])
            dve.tensor_scalar(tile_row[:, :], map_out[1], float(PAD_AT), None, ALU.add).then_inc(map_ready, 1)
            dve.wait_ge(map_ready, 1)
            dve.wait_ge(w_moe_loaded, 48)
            now, late = [], []

            def tile(j, s, turn):
                if s == 0:
                    now[:] = load_many(dve, expert_now, SLOTS * turn, SLOTS, 0, E - 1)
                    late[:] = load_many(dve, expert_late, SLOTS * turn, SLOTS, 0, E - 1)
                n, k = j - AT_W2, (s - AT_W2) % SLOTS
                if in_range(n):
                    dve.wait_ge(y_done, n + 1)
                    dve.tensor_tensor(y_biased_s[:, k % 2, :], expert_out[k % 2],
                                      b2_s[:, ds(late[s], 1), :].rearrange("p o d -> p (o d)"), ALU.add).then_inc(y_biased, 1)
                if in_range(j):
                    need(dve, hid_ready, j - BUFS + 1)
                    dve.tensor_copy(w1_e[:, s % BUFS, :], w1x_s[:, ds(now[s], 1), :].rearrange("p o f -> p (o f)")).then_inc(w1_ready, 1)
                if in_range(n):
                    dve.wait_ge(y_biased, n + 1)
                    dve.tensor_tensor(y_gated_s[:, k % 2, :], y_biased_s[:, k % 2, :], rows_in[k][:, GW:GW + D],
                                      ALU.mult).then_inc(y_gated, 1)
                n, k = j - AT_OUT, (s - AT_OUT) % SLOTS
                if in_range(n):
                    dve.wait_ge(y_gated, n + 1)
                    dve.tensor_tensor(out_s[k][:, :], y_gated_s[:, k % 2, :], rows_in[k][:, X2:X2 + D], ALU.add).then_inc(out_ready, 1)

            over_tiles(dve, tile, AT_OUT)


def _laid_out(inp):
    import numpy as np

    w_in = inp["L0_attn_w_in"].reshape(H, 3, DH, D)
    b_in = inp["L0_attn_b_in"].reshape(H, 3, DH)
    w1 = inp["L0_ffn_w1"].transpose(1, 0, 2)
    b1 = inp["L0_ffn_b1"].reshape(E, FH, P).transpose(2, 0, 1)
    experts = np.arange(E)
    arrays = {
        "x": inp["L0_attn_x"],
        "w_qkv": w_in.transpose(3, 1, 0, 2).reshape(D, 3, D),
        "b_qk": b_in[:, 0:2].transpose(0, 2, 1).reshape(D, 2),
        "b_v": b_in[:, 2].reshape(1, D),
        "w_out": inp["L0_attn_w_out"].T,
        "b_out": inp["L0_attn_b_out"].reshape(1, D),
        "router_w": inp["L0_ffn_router_w"],
        "w1x": np.concatenate([w1, b1], axis=2),
        "w2": inp["L0_ffn_w2"].reshape(E, FH, P, D).transpose(2, 0, 1, 3),
        "b2": inp["L0_ffn_b2"].reshape(1, E * D),
        "c_t": inp["L0_c"].T,
        "wmod": inp["L0_wmod"],
        "ident": np.eye(P, dtype=np.float32),
        "before": np.triu(np.ones((P, P)), 1).astype(np.float32),
        "expert_row": np.concatenate([E - experts, experts, experts * ROOM]).astype(np.float32).reshape(1, 3 * E),
        "first_row": (experts * ROOM).astype(np.float32).reshape(1, E),
        "tile_numbers": np.stack([P * np.arange(NT) - PAD_AT, np.arange(NT)], axis=1).astype(np.float32),
        "token_numbers": np.arange(-L, 0, dtype=np.int32).reshape(LT, P).T,
    }
    return {k: np.ascontiguousarray(v) for k, v in arrays.items()}


def kernel(**inputs):
    import concourse.bacc as _bacc
    import numpy as _np
    from concourse.bass_utils import run_bass_kernel_spmd as _run

    arrays = _laid_out({k: _np.asarray(v) for k, v in inputs.items()})
    nc = _bacc.Bacc("TRN2", target_bir_lowering=False, num_devices=1)
    feeds, args = {}, []
    for name, a in arrays.items():
        feeds[f"in_{name}_dram"] = a
        args.append(nc.dram_tensor(f"in_{name}_dram", a.shape, mybir.dt.from_np(a.dtype), kind="ExternalInput").ap())
    args.append(nc.dram_tensor("out_0_dram", (B, L, D), F32, kind="ExternalOutput").ap())
    build_adaln_attention_moe(nc, *args)
    r = _run(nc, [feeds], core_ids=[0])
    return r.results[0]["out_0_dram"]
```
